# Optimizing a Trainium2 kernel written in Bass

```python
import numpy as np
import jax
import jax.numpy as jnp

def _softmax(x, axis=-1):
    return jax.nn.softmax(x, axis=axis)

def _gelu(x):
    return jax.nn.gelu(x, approximate=True)

def _silu(x):
    return jax.nn.silu(x)

def _sigmoid(x):
    return jax.nn.sigmoid(x)

def _layernorm(x, axis=-1, eps=1e-05):
    m = jnp.mean(x, axis=axis, keepdims=True)
    v = jnp.var(x, axis=axis, keepdims=True)
    return (x - m) / jnp.sqrt(v + eps)

def _scatter_add(tgt, idx, src, axis=0):
    return tgt.at[idx].add(src)

def _segment_sum(src, seg, n):
    return jax.ops.segment_sum(src, seg, n)
kernel_name = 'mk_recurrent_d1_jaxref_r8_28b398'

def setup_inputs(seed: int=0):
    np.random.seed(seed)
    _w = jnp.asarray

    def _L0_attn_setup():
        import jax, jax.numpy as jnp
        import numpy as np
        H = 16
        G = 4
        DIM = 128
        HD = DIM // H // G
        key = jax.random.key(seed)
        k1, k2, k3 = jax.random.split(key, 3)
        x = jax.random.normal(k1, (8, 512, DIM), dtype=jnp.float32)
        w_qkvw = jax.random.normal(k2, (DIM, 4 * DIM), dtype=jnp.float32) * 0.02
        w_out = jax.random.normal(k3, (DIM, DIM), dtype=jnp.float32) * 0.02
        return {'x': x, 'w_qkvw': w_qkvw, 'w_out': w_out}
    _L0_attn_in = _L0_attn_setup()

    def _L0_ffn_setup():
        import jax, jax.numpy as jnp
        import numpy as np
        B, S, D, F, E = (1, 128, 128, 512, 8)
        EPS = 1e-05

        def _sublayer(xs, g, b, W1e, b1e, W2e, b2e):
            mu = jnp.mean(xs, axis=-1, keepdims=True)
            var = jnp.mean(jnp.square(xs - mu), axis=-1, keepdims=True)
            h = (xs - mu) * jax.lax.rsqrt(var + EPS) * g + b
            return xs + jax.nn.relu(h @ W1e.T + b1e) @ W2e.T + b2e
        key = jax.random.key(seed)
        ks = jax.random.split(key, 4)
        x = jax.random.normal(ks[0], (B, S, D), jnp.float32)
        centroids = jax.random.normal(ks[1], (E, D), jnp.float32) * 0.1
        gamma = jnp.ones((E, D), jnp.float32)
        beta = jnp.zeros((E, D), jnp.float32)
        W1 = jax.random.normal(ks[2], (E, F, D), jnp.float32) * 0.02
        b1 = jnp.zeros((E, F), jnp.float32)
        W2 = jax.random.normal(ks[3], (E, D, F), jnp.float32) * 0.02
        b2 = jnp.zeros((E, D), jnp.float32)
        return {'x': x, 'centroids': centroids, 'gamma': gamma, 'beta': beta, 'W1': W1, 'b1': b1, 'W2': W2, 'b2': b2}
    _L0_ffn_in = _L0_ffn_setup()
    _d = {'L0_attn_x': _L0_attn_in['x'], 'L0_attn_w_qkvw': _L0_attn_in['w_qkvw'], 'L0_attn_w_out': _L0_attn_in['w_out'], 'L0_ffn_centroids': _L0_ffn_in['centroids'], 'L0_ffn_gamma': _L0_ffn_in['gamma'], 'L0_ffn_beta': _L0_ffn_in['beta'], 'L0_ffn_W1': _L0_ffn_in['W1'], 'L0_ffn_b1': _L0_ffn_in['b1'], 'L0_ffn_W2': _L0_ffn_in['W2'], 'L0_ffn_b2': _L0_ffn_in['b2']}
    _x0 = _d['L0_attn_x']
    _d['L0_attn_x'] = jax.random.normal(jax.random.fold_in(jax.random.key(seed), 1), (32, 256, 128), dtype=_x0.dtype)
    del _x0
    return _d

def reference(L0_attn_x, L0_attn_w_qkvw, L0_attn_w_out, L0_ffn_centroids, L0_ffn_gamma, L0_ffn_beta, L0_ffn_W1, L0_ffn_b1, L0_ffn_W2, L0_ffn_b2):

    def _L0_attn_ref(x, w_qkvw, w_out):
        import jax, jax.numpy as jnp
        import numpy as np
        H = 16
        G = 4
        DIM = 128
        HD = DIM // H // G
        B, S, dim = x.shape
        qkvw = x @ w_qkvw
        chunks = jnp.split(qkvw, G, axis=-1)
        subs = [jnp.split(t, G, axis=-1) for t in chunks]
        q = jnp.concatenate([subs[i][0] for i in range(4)], axis=0)
        k = jnp.concatenate([subs[i][1] for i in range(4)], axis=0)
        v = jnp.concatenate([subs[i][2] for i in range(4)], axis=0)
        w = jnp.concatenate([subs[i][3] for i in range(4)], axis=0)

        def shp(t):
            return t.reshape(B * G, H, -1, HD).swapaxes(1, 2)
        q, k, v = (shp(q), shp(k), shp(v))
        w = w.reshape(B * G, H, -1, HD)
        scale = HD ** (-0.5)
        scores = q @ k.swapaxes(-2, -1) * scale
        attn = jax.nn.softmax(scores, axis=-1)
        o = (attn @ v).swapaxes(1, 2).reshape(B, S, dim)
        return o * w.reshape(B, S, dim) @ w_out

    def _L0_ffn_ref(x, centroids, gamma, beta, W1, b1, W2, b2):
        import jax, jax.numpy as jnp
        import numpy as np
        B, S, D, F, E = (1, 128, 128, 512, 8)
        EPS = 1e-05

        def _sublayer(xs, g, b, W1e, b1e, W2e, b2e):
            mu = jnp.mean(xs, axis=-1, keepdims=True)
            var = jnp.mean(jnp.square(xs - mu), axis=-1, keepdims=True)
            h = (xs - mu) * jax.lax.rsqrt(var + EPS) * g + b
            return xs + jax.nn.relu(h @ W1e.T + b1e) @ W2e.T + b2e
        feats = x.reshape(-1, x.shape[-1])
        scores = jax.lax.stop_gradient(feats @ centroids.T)
        expert = jnp.argmax(scores, axis=1)
        onehot = jax.nn.one_hot(expert, E, dtype=feats.dtype)
        alpha = jax.nn.sigmoid(jnp.sum(feats * centroids[expert], axis=-1, keepdims=True))
        ys = jax.vmap(_sublayer, in_axes=(None, 0, 0, 0, 0, 0, 0))(feats, gamma, beta, W1, b1, W2, b2)
        y = jnp.einsum('te,etd->td', onehot, ys)
        out = alpha * y + (1.0 - alpha) * feats
        return out.reshape(x.shape)
    x = L0_attn_x
    xn = _layernorm(x, axis=-1)
    s = _L0_attn_ref(xn, L0_attn_w_qkvw, L0_attn_w_out)
    g = _silu(_L0_ffn_ref(xn, L0_ffn_centroids, L0_ffn_gamma, L0_ffn_beta, L0_ffn_W1, L0_ffn_b1, L0_ffn_W2, L0_ffn_b2))
    x = x + s * g
    return x

_drawn_inputs = setup_inputs


def setup_inputs(seed=0):
    import zlib

    import numpy as np

    out = dict(_drawn_inputs(seed))
    spreads = {'L0_ffn_gamma': (1.0, 0.6),
     'L0_ffn_beta': (0.0, 0.8),
     'L0_ffn_b1': (0.0, 0.8),
     'L0_ffn_b2': (0.0, 0.8)}
    factors = {'L0_attn_w_qkvw': 8.0,
     'L0_attn_w_out': 8.0,
     'L0_ffn_centroids': 8.0,
     'L0_ffn_W1': 8.0,
     'L0_ffn_W2': 8.0}
    for name, (base, spread) in spreads.items():
        noise = np.random.default_rng([zlib.crc32(name.encode()), seed]).standard_normal(out[name].shape)
        drawn = base * np.exp(spread * noise) if base else spread * noise
        out[name] = jnp.asarray(drawn.astype(out[name].dtype))
    for name, factor in factors.items():
        out[name] = (out[name] * factor).astype(out[name].dtype)
    return out
```

```python
from contextlib import ExitStack

import concourse.bass as bass
from concourse import mybir

F32 = mybir.dt.float32
BF16 = mybir.dt.bfloat16
I32 = mybir.dt.int32
U32 = mybir.dt.uint32
ALU = mybir.AluOpType
ACT = mybir.ActivationFunctionType
AX_X = mybir.AxisListType.X

P = 128
D = 128
B, S = 32, 256
NT = B * S // P
H = 16
NI = 4
NR = 4
C = D // NI
NP = C // 2
SCALE = 2.0 ** -0.5
EPS = 1e-5

E = 8
F = 512
FC = F // P
FT = 72
FTL = FT + 4
W1C = F + FC

GT = 8
NG = NT // GT

NBG = 4
BGT = NT // NBG
HP = NP // 2
N = HP * H
SZ = H * N
NQ = 2 * NI
FFN_BGS = (1, 2)
PER_BG = FT // len(FFN_BGS)
FFN_STEPS = [5, 4] * 4
ZERO_DMAS = -(-FTL * D // SZ)


class Count:

    def __init__(self, sem):
        self.sem, self.n, self.base = sem, 0, 0

    def inc(self, ins):
        ins.then_inc(self.sem, 1)
        self.n += 1

    def wait(self, eng):
        eng.wait_ge(self.sem, self.base + self.n)

    def step(self, eng, ins):
        self.inc(ins)
        self.wait(eng)

    def turn(self, it, per):
        self.start, self.per, self.base = self.n, per, it * per

    def left(self, turns):
        assert self.n - self.start == self.per, (self.n - self.start, self.per)
        self.n, self.base = self.start + turns * self.per, 0


def work_uses(bg, last):
    uses = []
    for q in range(NQ):
        m = q // 2
        if q == 4 and not last:
            uses += [(q, "xT", bg + 1, j) for j in range(4)]
        if q % 2 == 1 and (m < 2 or not last):
            uses += [(q, "qkvw", bg * NI + m + 2, j) for j in range(4)]
    return uses + [(NQ, "oT", bg, j) for j in range(4)]


def program(nc, x, w_qkvw, w_out, centroids, gamma, beta, W1, b1, W2, b2, out):
    with ExitStack() as ctx:
        def sb(name, shape, dt=F32):
            return ctx.enter_context(nc.sbuf_tensor(name, shape, dt))

        def sem(name):
            return ctx.enter_context(nc.semaphore(name))

        xs_dram = nc.dram_tensor("xs_dram", [FTL * P, D], F32, kind="Internal").ap()
        y_dram = nc.dram_tensor("y_dram", [FT * P, D], F32, kind="Internal").ap()

        xf = x.rearrange("b s d -> (b s) d")
        outf = out.rearrange("b s d -> (b s) d")

        A = sb("A", [P, SZ])
        Bb = sb("Bb", [P, SZ])
        EXY = sb("EXY", [P, 2, 3, SZ])
        QK = sb("QK", [P, 2, 2, 2, NP, H])
        VW = sb("VW", [P, NI, 2, 2, NP, H])
        x_bg = sb("x_bg", [P, BGT, D])
        xnT = sb("xnT", [P, BGT * P])
        OO = sb("OO", [P, 2 * H * D])
        OJ = x_bg[:, :, :].rearrange("p (i k) d -> p i (k d)", i=NI)
        O = OO[:, 0:H * D].rearrange("p (h c) -> p h c", h=H)
        OT = OO[:, H * D:]
        xhat = sb("xhat", [P, NT * D])
        s_all = xhat
        WW = sb("WW", [P, E * W1C + E * F])
        W1s = WW[:, 0:E * W1C]
        W2s = WW[:, E * W1C:]
        f_all = WW[:, 0:NT * D]
        w1slot = sb("w1slot", [P, 2, W1C])
        xs = sb("xs", [P, 2, D])
        xsT = sb("xsT", [P, 2, P])
        hT = sb("hT", [P, 2, FC, P])
        ysb = sb("ysb", [P, 2, D])
        wq = sb("wq", [P, NI * NR * C])
        wo = sb("wo", [P, D])
        ident = sb("ident", [P, P])
        perm = sb("perm", [P, P])
        tri = sb("tri", [P, P], BF16)
        onesb = sb("onesb", [P, P], BF16)
        row0 = sb("row0", [P, P])
        eps = sb("eps", [P, 1])
        b2row = sb("b2row", [P, E * D])
        small = OO[0:3 * E + E * FC, 3136:3136 + D]
        smallT = sb("smallT", [P, 3 * E + E * FC])
        cT, gT, bT = (smallT[:, E * n:E * n + E] for n in range(3))
        b1T = smallT[:, 3 * E:]
        RS = sb("RS", [P, NT])
        NM = sb("NM", [P, NT])
        alpha = sb("alpha", [P, NT])
        slot = sb("slot", [P, NT], U32)
        ids = sb("ids", [P, FTL], I32)
        rden = sb("rden", [P, N])
        idle = sb("idle", [P, 1])
        osb = sb("osb", [P, 2, N])
        tot_i = sb("tot_i", [P, E], I32)
        tile_no, ids_f = OO[:, 3264:3264 + FTL], OO[:, 3392:3392 + FTL]

        flat = EXY[:, :, :, :].rearrange("p a b n -> p (a b n)")
        w1raw = flat[:, 0:E * F].rearrange("p (m d) -> p m d", d=D)
        w2raw = flat[:, E * F:2 * E * F].rearrange("p (e f) -> p e f", f=F)
        G = GT * D
        x_st = [flat[:, 8192 + n * G:8192 + (n + 1) * G].rearrange("p (k d) -> p k d", k=GT) for n in range(3)]
        xn_st = [v.rearrange("p (k d) -> p k d", k=GT) for v in (A[:, 0:G], A[:, G:2 * G], flat[:, 8192 + 3 * G:8192 + 4 * G])]
        xnT_g = QK[:, :, :, :, :, :].rearrange("p a b c r h -> p (a b c r h)")[:, 0:GT * P]
        zeros = Bb
        scores = OO[:, 0:512].rearrange("p (t e) -> p t e", e=E)
        eq = OO[:, 512:1024].rearrange("p (t e) -> p t e", e=E)
        oh = OO[:, 1024:1536].rearrange("p (t e) -> p t e", e=E)
        cum = [OO[:, 1536 + 512 * n:2048 + 512 * n].rearrange("p (t e) -> p t e", e=E) for n in range(2)]
        rt = OO[:, 2560:2560 + 5 * NT].rearrange("p (n t) -> p n t", n=5)
        ohb = OO[:, 2880:3136].bitcast(BF16)
        st = OO[:, 3472:3472 + 6 * GT].rearrange("p (k n) -> p k n", n=6)
        mv = OO[:, 3520:3520 + 6 * GT].rearrange("p (s k n) -> p s k n", s=3, n=2)
        dev, rs, nm, sq, dev2, rs2 = (OO[:, c:c + 3 * GT].rearrange("p (s k) -> p s k", s=3)
                                      for c in range(3568, 3568 + 18 * GT, 3 * GT))
        r8 = OO[:, 3712:3712 + 8 * E].rearrange("p (n e) -> p n e", e=E)

        bank = [ctx.enter_context(nc.psum_tensor(f"bank{n}", [P, 512], F32)) for n in range(8)]
        work = bank[0:2]
        sums = bank[2:4]
        hT_ps, xsT_ps, y_ps, out_ps = bank[4:8]

        small_in, w_in, wraw_in = sem("small_in"), sem("w_in"), sem("wraw_in")
        x_in = [sem(f"x_in{n}") for n in range(3)]
        zeroed, scattered = sem("zeroed"), sem("scattered")
        gathered = [sem("gathered_first"), sem("gathered_rest")]
        consts, dve_own = sem("consts"), sem("dve_own")
        pool_own = sem("pool_own")
        smallT_ps, smallT_ready = sem("smallT_ps"), sem("smallT_ready")
        var1, dev1, var2, dev_2 = sem("var1_ready"), sem("dev1_ready"), sem("var2_ready"), sem("dev2_ready")
        fold_ready = sem("fold_ready")
        xn_ready, xnT_ps, xnT_sb = sem("xn_ready"), sem("xnT_ps"), sem("xnT_sb")
        sc_ps, sc_ready = sem("sc_ps"), sem("sc_ready")
        oh_ready, prefix_ps, mx_ready, emx_ready = sem("oh_ready"), sem("prefix_ps"), sem("mx_ready"), sem("emx_ready")
        route_ready, xhat_ready = sem("route_ready"), sem("xhat_ready")
        wT_ps, wT_ready, b1_ps, w1_ready = sem("wT_ps"), sem("wT_ready"), sem("b1_ps"), sem("w1_ready")
        xbg_in, xnb_ready = sem("xbg_in"), sem("xnb_ready")
        filled = {k: sem(k + "_ps") for k in ("qkvw", "xT", "oT")}
        ready = {k: sem(k + "_ready") for k in ("qkvw", "xT", "oT")}
        vw_ready = sem("vw_ready")
        s_ready, exp_ready = sem("s_ready"), sem("exp_ready")
        ev0_ready, ev1_ready = sem("ev0_ready"), sem("ev1_ready")
        sum_ready, f_ready = sem("sum_ready"), sem("f_ready")
        proj_ps, proj_ready, oj_in = sem("proj_ps"), sem("proj_ready"), sem("oj_in")
        xs_in = [sem("xs_in0"), sem("xs_in1")]
        w1_in = [sem("w1_in0"), sem("w1_in1")]
        y_out = [sem("y_out0"), sem("y_out1")]
        xsT_full, xsT_ready = sem("xsT_full"), sem("xsT_ready")
        h_full, h_ready = sem("h_full"), sem("h_ready")
        y_full, y_ready = sem("y_full"), sem("y_ready")
        fx_in = [sem(f"fx_in{i}") for i in range(NI)]
        sg_ready = sem("sg_ready")
        fxn_ready, z_ready, g_ready, res_ready = sem("fxn_ready"), sem("z_ready"), sem("g_ready"), sem("res_ready")
        res_out = [sem(f"res_out{i}") for i in range(NI)]

        block = ctx.enter_context(nc.Block())

        def bgs(eng, body):
            body(0, None)
            with eng.Fori(0, len(FFN_BGS)) as turn:
                body(turn + FFN_BGS[0], turn)
            body(NBG - 1, None)

        def groups(eng, step):
            step(0, 0, 0)
            with eng.Fori(0, (NG - 2) // 3) as it:
                for j in range(1, 4):
                    step(it * 3 + j, j % 3, it + j // 3)
            step(NG - 1, (NG - 1) % 3, (NG - 1) // 3)

        def ffn_tiles(turn):
            k, steps = 0, []
            for n in FFN_STEPS:
                steps.append([(turn * PER_BG + k + j, turn * (PER_BG // 2), k + j) for j in range(n)])
                k += n
            return steps

        NF = 4 * D
        qk_flat = QK[:, :, :, :, :, :].rearrange("p a b c r h -> p (a b c r h)")
        fin_x, fin_z, fin_n, fin_r = ([buf[:, i * NF:(i + 1) * NF] for i in range(NI)] for buf in (xnT, A, Bb, qk_flat))

        def fin_rows(ap, bg, i):
            t0 = i * BGT + bg * 4
            return ap[bass.ds(t0 * P, NF // D * P), :].rearrange("(k p) d -> p k d", p=P)

        @block.sync
        def _(sp):
            def load_x(g, s):
                sp.dma_start(x_st[s], xf[bass.ds(g * (GT * P), GT * P), :].rearrange("(k p) d -> p k d", p=P))\
                    .then_inc(x_in[s], 16)

            for g in range(3):
                load_x(g, g)
            sp.dma_start(wq[:, :], w_qkvw).then_inc(w_in, 16)
            sp.dma_start(wo[:, :], w_out).then_inc(w_in, 16)
            sp.wait_ge(consts, 7)
            sp.dma_start(b2row[0:1, :], b2.rearrange("(a e) d -> a (e d)", a=1)).then_inc(w_in, 16)
            for g in range(3, NG):
                sp.wait_ge(xn_ready, g - 2)
                load_x(g, g % 3)

            def load_bg(bg):
                for k in range(0, BGT, GT):
                    sp.dma_start(x_bg[:, k:k + GT, :], xf[bass.ds(bg * (BGT * P) + k * P, GT * P), :]
                                 .rearrange("(k p) d -> p k d", p=P)).then_inc(xbg_in, 16)

            load_bg(0)

            def load_xs(k, half, j):
                sp.dma_start(xs[:, j % 2, :], xs_dram[bass.ds(k * P, P), :]).then_inc(xs_in[j % 2], 16)

            def load_w1(k, half, j):
                e = sp.value_load(ids[0:1, bass.ds(k, 1)], min_val=0, max_val=E - 1)
                sp.dma_start(w1slot[:, j % 2, :], W1s[:, bass.ds(e * W1C, W1C)]).then_inc(w1_in[j % 2], 16)

            for s in range(2):
                sp.sem_inc(y_out[s], 16)
            for i in range(NI):
                sp.sem_inc(res_out[i], 16)

            def body(bg, turn):
                if turn is None and bg == NBG - 1:
                    return
                if turn is None:
                    sp.wait_ge(filled["xT"], 4)
                    load_bg(1)
                    sp.wait_ge(route_ready, 2)
                    sp.wait_ge(w1_ready, 2)
                    sp.wait_ge(scattered, 16 * NT)
                    for k in range(2):
                        load_xs(k, 0, k)
                        load_w1(k, 0, k)
                    for k in range(2, 4):
                        sp.wait_ge(xsT_full, k - 1)
                        load_xs(k, 0, k)
                    sp.wait_ge(h_ready, FC)
                    load_w1(2, 0, 2)
                    return
                for q, steps in enumerate(ffn_tiles(turn)):
                    if q == 2:
                        sp.wait_ge(proj_ps, bg * NI)
                        load_bg(bg + 1)
                    for k, half, j in steps:
                        sp.wait_ge(xsT_full, k + 3)
                        load_xs(k + 4, half, j + 4)
                        sp.wait_ge(h_ready, (k + 2) * FC)
                        load_w1(k + 3, half, j + 3)
                        sp.wait_ge(y_ready, k + 2)
                        sp.dma_start(y_dram[bass.ds(k * P, P), :], ysb[:, j % 2, :]).then_inc(y_out[j % 2], 16)

            bgs(sp, body)

            def load_fin(bg, i):
                sp.dma_start(fin_x[i].rearrange("p (k d) -> p k d", d=D), fin_rows(xf, bg, i)).then_inc(fx_in[i], 16)

            def store_fin(bg, i):
                sp.wait_ge(res_ready, bg * NI + i + 1)
                sp.dma_start(fin_rows(outf, bg, i), fin_r[i].rearrange("p (k d) -> p k d", d=D))\
                    .then_inc(res_out[i], 16)

            sp.wait_ge(filled["qkvw"], NBG * NI * 4)
            for i in range(NI):
                load_fin(0, i)
            with sp.Fori(0, NBG - 1) as bg:
                for i in range(NI):
                    store_fin(bg, i)
                    load_fin(bg + 1, i)
            for i in range(NI):
                store_fin(NBG - 1, i)
            for i in range(NI):
                sp.wait_ge(res_out[i], 16 * (1 + NBG))

        @block.gpsimd
        def _(pool):
            own = Count(pool_own)
            own.inc(pool.memset(ident[:, :], 0.0))
            own.inc(pool.memset(tri[:, :], 1.0))
            pool.memset(onesb[:, :], 1.0).then_inc(consts, 1)
            own.inc(pool.memset(row0[:, :], 0.0))
            own.inc(pool.memset(b2row[:, :], 0.0))
            pool.memset(eps[:, :], EPS).then_inc(consts, 1)
            own.wait(pool)
            pool.affine_select(out=ident[:, :], in_=ident[:, :], compare_op=ALU.not_equal, fill=1.0, base=0,
                               pattern=[[-1, P]], channel_multiplier=1).then_inc(consts, 1)
            pool.memset(row0[0:1, :], 1.0).then_inc(consts, 1)
            pool.wait_ge(consts, 4)
            pool.tensor_copy(perm[:, :].rearrange("p (j m) -> p j m", j=4),
                             ident[:, :].rearrange("p (m j) -> p j m", j=4)).then_inc(consts, 1)
            pool.affine_select(out=tri[:, :], in_=tri[:, :], compare_op=ALU.is_gt, fill=0.0, base=0,
                               pattern=[[1, P]], channel_multiplier=-1).then_inc(consts, 1)
            pool.iota(tile_no[:, :], [[1, FTL]], base=0, channel_multiplier=0,
                      allow_small_or_imprecise_dtypes=True).then_inc(consts, 1)
            own.step(pool, pool.memset(zeros[:, :], 0.0))
            flat_xs = xs_dram.rearrange("(p r) d -> p (r d)", p=P)
            per, at = FTL * D, 0
            while at < per:
                n = min(SZ, per - at)
                pool.dma_start(flat_xs[:, at:at + n], zeros[:, 0:n]).then_inc(zeroed, 16)
                at += n
            pool.wait_ge(zeroed, 16 * ZERO_DMAS)

            def scatter(t):
                pool.indirect_dma_start(out=xs_dram, out_offset=bass.IndirectOffsetOnAxis(ap=slot[:, t:t + 1], axis=0),
                                        in_=xhat[:, t * D:(t + 1) * D], in_offset=None).then_inc(scattered, 16)

            def ev1(n, q):
                if q % 2 == 0:
                    pool.wait_ge(vw_ready, n * 2 + 4)
                pool.wait_ge(exp_ready, n + 1)
                if not (isinstance(n, int) and n < 2):
                    pool.wait_ge(sum_ready, n - 1)
                m, p0 = q // 2, HP * (q % 2)
                pool.tensor_tensor(
                    EXY[:, q % 2, 2, :].rearrange("p (g r h) -> p g r h", g=H, h=H),
                    EXY[:, q % 2, 0, :].rearrange("p (g r h) -> p g r h", g=H, h=H),
                    VW[:, m, 1, 0, p0:p0 + HP, :].rearrange("p r g -> p g r").unsqueeze(3).broadcast_to([P, H, HP, H]),
                    ALU.mult).then_inc(ev1_ready, 1)

            def fold1(n, q):
                pool.wait_ge(ev1_ready, n + 1)
                lo, hi = EXY[:, q % 2, 2, 0:SZ // 2], EXY[:, q % 2, 2, SZ // 2:]
                pool.tensor_tensor(lo, lo, hi, ALU.add).then_inc(fold_ready, 1)

            ev1(0, 0)
            pool.wait_ge(route_ready, 1)
            pool.wait_ge(xhat_ready, NG)

            def body(bg, turn):
                first, last = turn is None and bg == 0, turn is None and bg == NBG - 1
                for q in range(NQ):
                    if not (last and q == NQ - 1):
                        ev1(bg * NQ + q + 1, (q + 1) % NQ)
                    if turn is not None:
                        fold1(bg * NQ + q + 1, (q + 1) % NQ)
                    if first:
                        for t in range(min(q * 11, NT), min(q * 11 + 11, NT)):
                            scatter(t)
                    if last:
                        if q == 0:
                            for s in range(2):
                                pool.wait_ge(y_out[s], 16 * (1 + FT // 2))
                            pool.wait_ge(h_full, FT + 1)
                            for s in range(2):
                                pool.wait_ge(w1_in[s], 16 * ((FT + 4) // 2 - s))
                        order = [i * BGT + b * 4 + k for b in range(NBG) for i in range(NI) for k in range(4)]
                        for m in range(min(q * 11, NT), min(q * 11 + 11, NT)):
                            t = order[m]
                            pool.indirect_dma_start(out=f_all[:, t * D:(t + 1) * D], out_offset=None, in_=y_dram,
                                                    in_offset=bass.IndirectOffsetOnAxis(ap=slot[:, t:t + 1], axis=0))\
                                .then_inc(gathered[m >= BGT], 16)

            bgs(pool, body)

            with pool.Fori(0, NBG) as bg:
                for i in range(NI):
                    w = bg * NI + i
                    pool.wait_ge(g_ready, w + 1)
                    pool.wait_ge(res_out[i], (bg + 1) * 16)
                    pool.tensor_tensor(fin_r[i], fin_z[i], fin_x[i], ALU.add).then_inc(res_ready, 1)

        @block.scalar
        def _(act):
            for n, w in enumerate((centroids, gamma, beta)):
                act.dma_start(small[E * n:E * n + E, :], w).then_inc(small_in, 16)
            act.dma_start(small[3 * E:, :], b1.rearrange("e (c f) -> (e c) f", c=FC)).then_inc(small_in, 16)
            act.wait_ge(smallT_ps, 1)
            act.activation(smallT[:, :], work[0][:, 0:3 * E + E * FC], ACT.Copy).then_inc(smallT_ready, 1)

            act.wait_ge(consts, 7)

            def deviation(g, s):
                act.wait_ge(var1, g + 1)
                act.activation(dev[:, s, :], mv[:, s, :, 1], ACT.Sqrt, bias=eps[:, 0:1]).then_inc(dev1, 1)

            def group(g, s, first=False):
                act.wait_ge(var2, g + 1)
                act.activation(dev2[:, s, :], sq[:, s, :], ACT.Sqrt, bias=eps[:, 0:1]).then_inc(dev_2, 1)
                for j in range(2):
                    act.wait_ge(xnT_ps, g * 2 + j + 1)
                    if j == 0 and not first:
                        act.wait_ge(sc_ps, g)
                    act.activation(xnT_g[:, 512 * j:512 * j + 512], work[j][:, :], ACT.Copy).then_inc(xnT_sb, 1)
                act.wait_ge(sc_ps, g + 1)
                act.activation(scores[:, bass.ds(g * GT, GT), :].rearrange("p t e -> p (t e)"), out_ps[:, 0:GT * E],
                               ACT.Copy).then_inc(sc_ready, 1)

            deviation(0, 0)
            act.dma_start(w1raw, W1.rearrange("e (c p) d -> p (e c) d", p=P)).then_inc(wraw_in, 16)
            act.dma_start(w2raw, W2.rearrange("e n f -> n e f")).then_inc(wraw_in, 16)
            deviation(1, 1)
            group(0, 0, True)
            with act.Fori(0, (NG - 2) // 3) as it:
                for j in range(1, 4):
                    g = it * 3 + j
                    deviation(g + 1, (j + 1) % 3)
                    group(g, j % 3)
            group(NG - 1, (NG - 1) % 3)
            act.wait_ge(mx_ready, 1)
            act.activation(rt[:, 2, :], rt[:, 0, :], ACT.Exp, scale=-1.0).then_inc(emx_ready, 1)

            for u in range(2 * E):
                act.wait_ge(wT_ps, u + 1)
                e = u % E
                dst = W1s[:, e * W1C:e * W1C + F] if u < E else W2s[:, e * F:(e + 1) * F]
                act.activation(dst, work[u % 2][:, :], ACT.Copy).then_inc(wT_ready, 1)

            def normalise(bg):
                act.wait_ge(xbg_in, (bg + 1) * (16 * BGT // GT))
                for k in range(BGT):
                    t = bg * BGT + k
                    ins = act.activation(x_bg[:, k, :], x_bg[:, k, :], ACT.Identity, scale=RS[:, bass.ds(t, 1)],
                                         bias=NM[:, bass.ds(t, 1)])
                ins.then_inc(xnb_ready, 1)

            def evac(kind, n, j, u):
                act.wait_ge(filled[kind], n * 4 + j + 1)
                src = work[u % 2]
                if kind == "xT":
                    if not isinstance(n, int) or n:
                        act.wait_ge(filled["qkvw"], n * 4 * NI)
                    tok = xnT[:, :].rearrange("p (h b a) -> p b h a", h=H, a=H)
                    dst = tok[:, 2 * j:2 * j + 2, :, :]
                    src = src[:, :].rearrange("p (b h a) -> p b h a", b=2, h=H)
                elif kind == "oT":
                    if not isinstance(n, int) or n:
                        act.wait_ge(oj_in, n * (16 * NI * 4))
                    dst = OT.rearrange("p (m h a) -> p h m a", h=H, a=4)[:, 4 * j:4 * j + 4, :, :]
                    src = src[:, :].rearrange("p (h m a) -> p h m a", h=4, a=4)
                else:
                    i = evac.i
                    if not isinstance(n, int) or n >= 2:
                        act.wait_ge(s_ready, n * 2 - 2)
                    if not isinstance(n, int) or n >= NI:
                        act.wait_ge(f_ready, n * 2 - 6)
                    hh = H // 4
                    src = src[:, :].rearrange("p (h rc d) -> p d rc h", h=hh, d=2)
                    dst = VW[:, i, :, :, :, hh * j:hh * j + hh].rearrange("p d r c h -> p d (r c) h")
                    act.activation(dst, src[:, :, 2 * NP:, :], ACT.Copy).then_inc(vw_ready, 1)
                    dst = QK[:, i % 2, :, :, :, hh * j:hh * j + hh].rearrange("p d r c h -> p d (r c) h")
                    src = src[:, :, 0:2 * NP, :]
                act.activation(dst, src, ACT.Copy).then_inc(ready[kind], 1)

            def exp(n, q):
                act.wait_ge(s_ready, n + 1)
                if not (isinstance(n, int) and n < 2):
                    act.wait_ge(sum_ready, n - 1)
                act.activation(EXY[:, q % 2, 0, :], A[:, :], ACT.Exp, scale=SCALE).then_inc(exp_ready, 1)

            def evac_xsT(k, j):
                act.wait_ge(xsT_full, k + 1)
                if not (isinstance(k, int) and k < 2):
                    act.wait_ge(h_full, k - 1)
                act.activation(xsT[:, j % 2, :], xsT_ps[:, 0:P], ACT.Copy).then_inc(xsT_ready, 1)

            def relu(k, j):
                act.wait_ge(h_full, k + 1)
                if not (isinstance(k, int) and k < 2):
                    act.wait_ge(y_full, k)
                for c in range(FC):
                    act.activation(hT[:, j % 2, c, :], hT_ps[:, c * P:(c + 1) * P], ACT.Relu,
                                   bias=w1slot[:, j % 2, F + c:F + c + 1]).then_inc(h_ready, 1)

            def evac_y(k, half, j):
                act.wait_ge(y_full, k + 2)
                act.wait_ge(y_out[j % 2], (half + j // 2 + 1) * 16)
                act.activation(ysb[:, j % 2, :], y_ps[:, 0:D], ACT.Copy).then_inc(y_ready, 1)

            act.sem_inc(y_ready, 1)
            act.sem_inc(proj_ready, 1)
            normalise(0)
            act.wait_ge(b1_ps, 1)
            for e in range(E):
                ins = act.activation(W1s[:, e * W1C:e * W1C + F], W1s[:, e * W1C:e * W1C + F], ACT.Copy,
                                     scale=gT[:, e:e + 1])
            ins.then_inc(w1_ready, 1)
            for j in range(4):
                evac("xT", 0, j, j)
            for c in range(2):
                for j in range(4):
                    evac.i = c
                    evac("qkvw", c, j, j)
            act.wait_ge(wT_ps, 2 * E)
            exp(0, 0)
            exp(1, 1)

            def evac_proj(bg):
                act.wait_ge(scattered, 16 * NT)
                for i in range(NI):
                    w = bg * NI + i
                    act.wait_ge(proj_ps, w + 1)
                    act.activation(s_all[:, bass.ds(w * 512, 512)], out_ps[:, :], ACT.Copy).then_inc(proj_ready, 1)

            def body(bg, turn):
                first, last = turn is None and bg == 0, turn is None and bg == NBG - 1
                uses = work_uses(bg, last)
                ffn = ffn_tiles(turn) if turn is not None else [[]] * NQ
                for q in range(NQ + 1):
                    for u, (qq, kind, n, j) in enumerate(uses):
                        if qq == q:
                            evac.i = (q // 2 + 2) % NI
                            evac(kind, n, j, u)
                    if q == NQ:
                        act.wait_ge(ready["oT"], bg * 4 + 4)
                        if not isinstance(bg, int) or bg:
                            act.wait_ge(proj_ps, bg * NI)
                        for i in range(NI):
                            for j in range(4):
                                act.dma_start(OJ[C * j:C * j + C, i, :],
                                              OT[C * i:C * i + C, 4 * P * j:4 * P * (j + 1)]).then_inc(oj_in, 16)
                        if last:
                            evac_proj(bg)
                        break
                    if q == 1 and not first:
                        evac_proj(bg - 1)
                    for k, half, j in ffn[q][:2]:
                        evac_xsT(k + 2, j + 2)
                        relu(k + 1, j + 1)
                        evac_y(k, half, j)
                    if not last or q < NQ - 2:
                        exp(bg * NQ + q + 2, q)
                    for k, half, j in ffn[q][2:]:
                        evac_xsT(k + 2, j + 2)
                        relu(k + 1, j + 1)
                        evac_y(k, half, j)
                    if q == 3 and not last:
                        normalise(bg + 1)
                if turn is None and not last:
                    evac_xsT(0, 0)
                    evac_xsT(1, 1)
                    relu(0, 0)

            bgs(act, body)

            def fin_norm(bg, i):
                act.wait_ge(fx_in[i], (bg + 1) * 16)
                for k in range(2, 4):
                    t = bg * 4 + i * BGT + k
                    ins = act.activation(fin_n[i][:, k * D:(k + 1) * D], fin_x[i][:, k * D:(k + 1) * D],
                                         ACT.Identity, scale=RS[:, bass.ds(t, 1)], bias=NM[:, bass.ds(t, 1)])
                ins.then_inc(fxn_ready, 1)

            def gate(bg, i):
                act.wait_ge(z_ready, bg * NI + i + 1)
                act.activation(fin_z[i], fin_z[i], ACT.Silu).then_inc(sg_ready, 1)

            act.wait_ge(s_ready, NBG * NQ)
            fin_norm(0, 0)
            fin_norm(0, 1)
            with act.Fori(0, NBG - 1) as bg:
                for i in range(NI):
                    gate(bg, i)
                    fin_norm(bg + (i + 2) // NI, (i + 2) % NI)
            for i in range(NI):
                gate(NBG - 1, i)
                if i < 2:
                    fin_norm(NBG - 1, i + 2)

        @block.tensor
        def _(pe):
            pe.wait_ge(consts, 7)
            pe.wait_ge(small_in, 64)
            rows = 3 * E + E * FC
            pe.transpose(work[0][:, 0:rows], small[:, :], ident[0:rows, 0:rows]).then_inc(smallT_ps, 1)
            pe.wait_ge(smallT_ready, 1)

            def group(g, s, m):
                first = isinstance(g, int) and g == 0
                pe.wait_ge(xn_ready, g + 1)
                for j in range(2):
                    if not first:
                        pe.wait_ge(xnT_sb, g * 2 + j - 1)
                    for k in range(4):
                        ins = pe.transpose(work[j][:, k * P:(k + 1) * P], xn_st[s][:, 4 * j + k, :], ident[:, :])
                    ins.then_inc(xnT_ps, 1)
                if not first:
                    pe.wait_ge(sc_ready, g)
                for k in range(GT):
                    if k % 4 == 0:
                        pe.wait_ge(xnT_sb, g * 2 + k // 4 + 1)
                    ins = pe.matmul(out_ps[:, k * E:(k + 1) * E], xnT_g[:, k * P:(k + 1) * P], cT,
                                    start=True, stop=True)
                ins.then_inc(sc_ps, 1)

            groups(pe, group)
            pe.wait_ge(oh_ready, 1)
            pe.matmul(sums[0][:, :], tri[:, :], ohb[:, :], start=True, stop=True)
            pe.matmul(sums[1][:, :], onesb[:, :], ohb[:, :], start=True, stop=True).then_inc(prefix_ps, 1)

            pe.wait_ge(wraw_in, 32)
            pe.wait_ge(xnT_sb, 2 * NG)
            for u in range(2 * E):
                if u >= 2:
                    pe.wait_ge(wT_ready, u - 1)
                e = u % E
                for c in range(FC):
                    src = w1raw[:, e * FC + c, :] if u < E else w2raw[:, e, c * P:(c + 1) * P]
                    ins = pe.transpose(work[u % 2][:, c * P:(c + 1) * P], src, ident[:, :])
                ins.then_inc(wT_ps, 1)
            pe.wait_ge(sc_ready, NG)
            for m in range(E * FC):
                e, c = m // FC, m % FC
                ins = pe.matmul(out_ps[:, m:m + 1], W1s[:, e * W1C + c * P:e * W1C + (c + 1) * P], bT[:, e:e + 1],
                                start=True, stop=True)
            ins.then_inc(b1_ps, 1)

            def fill(kind, n, j, u):
                dst = work[u % 2]
                if kind == "xT":
                    if j == 0:
                        pe.wait_ge(xnb_ready, n + 1)
                    for k in range(4):
                        ins = pe.transpose(dst[:, k * P:(k + 1) * P], x_bg[:, 4 * j + k, :], ident[:, :])
                elif kind == "oT":
                    if j == 0:
                        pe.wait_ge(f_ready, n * NQ + NQ)
                    for k in range(4):
                        ins = pe.transpose(dst[:, k * P:(k + 1) * P], O[:, 4 * j + k, :], perm[:, :])
                else:
                    hh, tok = H // 4, xnT[:, :].rearrange("p (h n) -> p h n", h=H)
                    for h in range(hh):
                        ins = pe.matmul(dst[:, h * NR * C:(h + 1) * NR * C], tok[:, hh * j + h, :],
                                        wq[:, fill.i * NR * C:(fill.i + 1) * NR * C], start=True, stop=True)
                ins.then_inc(filled[kind], 1)

            def copied(kind, n, j):
                pe.wait_ge(ready[kind], n * 4 + j + 1)

            def sum_keys(n, q, turn=None, at=0):
                if turn is not None:
                    pe.wait_ge(fold_ready, turn * NQ + at + 1)
                pe.wait_ge(ev0_ready, n + 1)
                pe.wait_ge(ev1_ready, n + 1)
                if not (isinstance(n, int) and n < 2):
                    pe.wait_ge(f_ready, n - 1)
                keys = H if turn is None else H // 2
                for g in range(keys):
                    ins = pe.matmul(sums[q % 2][:, 0:3 * N], ident[:, :], EXY[:, q % 2, :, g * N:(g + 1) * N],
                                    start=(g == 0), stop=(g == keys - 1))
                ins.then_inc(sum_ready, 1)

            def ffn_transpose(k, half, j):
                pe.wait_ge(xs_in[j % 2], (half + j // 2 + 1) * 16)
                if not (isinstance(k, int) and k < 1):
                    pe.wait_ge(xsT_ready, k)
                pe.transpose(xsT_ps[:, 0:P], xs[:, j % 2, :], ident[:, :]).then_inc(xsT_full, 1)

            def ffn_up(k, half, j):
                pe.wait_ge(w1_in[j % 2], (half + j // 2 + 1) * 16)
                pe.wait_ge(xsT_ready, k + 1)
                if not (isinstance(k, int) and k < 1):
                    pe.wait_ge(h_ready, k * FC)
                for c in range(FC):
                    ins = pe.matmul(hT_ps[:, c * P:(c + 1) * P], w1slot[:, j % 2, c * P:(c + 1) * P],
                                    xsT[:, j % 2, :], start=True, stop=True)
                ins.then_inc(h_full, 1)

            def ffn_down(k, half, j):
                e = pe.value_load(ids[0:1, bass.ds(k, 1)], min_val=0, max_val=E - 1)
                pe.wait_ge(y_ready, k + 1)
                pe.matmul(y_ps[:, 0:D], row0[:, :], b2row[:, bass.ds(e * D, D)], start=True, stop=False)
                pe.wait_ge(h_ready, (k + 1) * FC)
                for c in range(FC):
                    ins = pe.matmul(y_ps[:, 0:D], hT[:, j % 2, c, :], W2s[:, bass.ds(e * F + c * P, D)],
                                    start=False, stop=(c == FC - 1))
                ins.then_inc(y_full, 1)

            pe.sem_inc(y_full, 1)
            pe.wait_ge(wT_ready, 2 * E)
            pe.wait_ge(w_in, 16 * 3)
            for j in range(4):
                if j >= 2:
                    copied("xT", 0, j - 2)
                fill("xT", 0, j, j)
            copied("xT", 0, 3)
            for c in range(2):
                for j in range(4):
                    if c or j >= 2:
                        copied("qkvw", (4 * c + j - 2) // 4, (j - 2) % 4)
                    fill.i = c
                    fill("qkvw", c, j, j)
            sum_ready_first = 0
            sum_keys(sum_ready_first, 0)

            def project(bg):
                pe.wait_ge(w1_ready, 2)
                for i in range(NI):
                    w = bg * NI + i
                    pe.wait_ge(oj_in, bg * (16 * NI * 4) + 16 * NI * 4)
                    pe.wait_ge(proj_ready, w + 1)
                    for b in range(4):
                        ins = pe.matmul(out_ps[:, b * D:(b + 1) * D], OJ[:, i, b * P:(b + 1) * P], wo[:, :],
                                        start=True, stop=True)
                    ins.then_inc(proj_ps, 1)

            def body(bg, turn):
                first, last = turn is None and bg == 0, turn is None and bg == NBG - 1
                uses = work_uses(bg, last)
                if isinstance(bg, int) and bg == 0:
                    before = [("qkvw", 1, 2), ("qkvw", 1, 3)]
                else:
                    before = [("oT", bg - 1, 2), ("oT", bg - 1, 3)]
                before += [(kind, n, j) for _, kind, n, j in uses]
                ffn = ffn_tiles(turn) if turn is not None else [[]] * NQ
                for q in range(NQ + 1):
                    for u, (qq, kind, n, j) in enumerate(uses):
                        if qq == q:
                            if kind == "qkvw":
                                fill.i = (q // 2 + 2) % NI
                                if fill.i == 0 and j == 0:
                                    pe.wait_ge(ready["xT"], bg * 4 + 8)
                            copied(*before[u])
                            fill(kind, n, j, u)
                    if q == NQ:
                        if last:
                            project(bg)
                        break
                    if q == 1 and not first:
                        project(bg - 1)
                    for k, half, j in ffn[q][:2]:
                        ffn_transpose(k + 2, half, j + 2)
                        ffn_up(k + 1, half, j + 1)
                        ffn_down(k, half, j)
                    if not last or q < NQ - 1:
                        sum_keys(bg * NQ + q + 1, q + 1, turn, q)
                    for k, half, j in ffn[q][2:]:
                        ffn_transpose(k + 2, half, j + 2)
                        ffn_up(k + 1, half, j + 1)
                        ffn_down(k, half, j)
                if turn is None and not last:
                    ffn_transpose(0, 0, 0)
                    ffn_transpose(1, 0, 1)
                    ffn_up(0, 0, 0)

            bgs(pe, body)

        @block.vector
        def _(dve):
            own = Count(dve_own)

            def stats(g, s, m):
                if not (isinstance(g, int) and g == 0):
                    dve.wait_ge(var1, g)
                dve.wait_ge(x_in[s], (m + 1) * 16)
                for k in range(GT):
                    ins = dve.bn_stats(st[:, k, :], x_st[s][:, k, :])
                own.step(dve, ins)
                dve.memset(idle[:, :], 0.0)
                for k in range(GT):
                    ins = dve.bn_aggr(mv[:, s, k, :], st[:, k, :])
                ins.then_inc(var1, 1)

            def norm(g, s, first=False):
                dve.wait_ge(dev1, g + 1)
                own.step(dve, dve.reciprocal(rs[:, s, :], dev[:, s, :]))
                own.inc(dve.scalar_tensor_tensor(out=nm[:, s, :], in0=mv[:, s, :, 0], scalar=-1.0, in1=rs[:, s, :],
                                                 op0=ALU.mult, op1=ALU.mult))
                own.step(dve, dve.tensor_tensor(sq[:, s, :], rs[:, s, :], rs[:, s, :], ALU.mult))
                dve.tensor_tensor(sq[:, s, :], sq[:, s, :], mv[:, s, :, 1], ALU.mult).then_inc(var2, 1)
                dve.tensor_copy(RS[:, bass.ds(g * GT, GT)], rs[:, s, :])
                dve.tensor_copy(NM[:, bass.ds(g * GT, GT)], nm[:, s, :])
                if not first:
                    dve.wait_ge(xnT_ps, g * 2 - 4)
                for k in range(GT):
                    ins = dve.tensor_scalar(xn_st[s][:, k, :], x_st[s][:, k, :], rs[:, s, k:k + 1], nm[:, s, k:k + 1],
                                            ALU.mult, ALU.add)
                ins.then_inc(xn_ready, 1)
                dve.wait_ge(dev_2, g + 1)
                own.step(dve, dve.reciprocal(rs2[:, s, :], dev2[:, s, :]))
                dve.wait_ge(xn_ready, g + 1)
                for k in range(GT):
                    ins = dve.tensor_scalar(xhat[:, bass.ds(g * (GT * D) + k * D, D)], xn_st[s][:, k, :],
                                            rs2[:, s, k:k + 1], None, ALU.mult)
                ins.then_inc(xhat_ready, 1)

            dve.wait_ge(consts, 7)
            stats(0, 0, 0)
            stats(1, 1, 0)
            norm(0, 0, True)
            stats(2, 2, 0)
            norm(1, 1, True)
            stats(3, 0, 1)
            norm(2, 2, True)
            with dve.Fori(1, (NG - 2) // 3) as it:
                own.turn(it - 1, 15)
                for j in range(1, 4):
                    stats(it * 3 + j, j % 3, it + j // 3)
                    norm(it * 3 + j - 1, (j - 1) % 3)
            own.left((NG - 2) // 3 - 1)
            stats(NG - 1, (NG - 1) % 3, (NG - 1) // 3)
            norm(NG - 2, (NG - 2) % 3)
            norm(NG - 1, (NG - 1) % 3)

            dve.wait_ge(sc_ready, NG)
            mx, emx, taken = rt[:, 0, :], rt[:, 2, :], rt[:, 1, :]
            dve.tensor_reduce(mx, scores, AX_X, ALU.max).then_inc(mx_ready, 1)
            dve.wait_ge(mx_ready, 1)
            own.inc(dve.memset(taken, 0.0))
            own.step(dve, dve.tensor_tensor(eq, scores, mx.unsqueeze(2).broadcast_to([P, NT, E]), ALU.is_ge))
            for e in range(E):
                own.inc(dve.tensor_tensor(oh[:, :, e], eq[:, :, e], taken, ALU.is_gt))
                own.step(dve, dve.tensor_tensor(taken, taken, eq[:, :, e], ALU.max))
            dve.tensor_copy(ohb[:, :], oh.rearrange("p t e -> p (t e)")).then_inc(oh_ready, 1)
            dve.wait_ge(prefix_ps, 1)
            in_tile = sums[0][:, :].rearrange("p (t e) -> p t e", e=E)
            of_tile = sums[1][:, :].rearrange("p (t e) -> p t e", e=E)
            own.step(dve, dve.tensor_copy(cum[0], of_tile))
            shift, at = 1, 0
            while shift < NT:
                src, dst = cum[at], cum[1 - at]
                own.inc(dve.tensor_copy(dst[:, 0:shift, :], src[:, 0:shift, :]))
                own.step(dve, dve.tensor_tensor(dst[:, shift:, :], src[:, shift:, :], src[:, 0:NT - shift, :], ALU.add))
                shift, at = 2 * shift, 1 - at
            upto = cum[at]
            own.step(dve, dve.tensor_scalar(tot_i[:, :], upto[:, NT - 1, :], float(P - 1), None, ALU.add))
            own.step(dve, dve.tensor_scalar(tot_i[:, :], tot_i[:, :], P.bit_length() - 1, None, ALU.logical_shift_right))
            tiles, ends, ends2, base = (r8[:, n, :] for n in range(4))
            own.step(dve, dve.tensor_copy(tiles, tot_i[:, :]))
            src, dst = tiles, ends
            for sh in (1, 2, 4):
                own.inc(dve.tensor_copy(dst[:, 0:sh], src[:, 0:sh]))
                own.step(dve, dve.tensor_tensor(dst[:, sh:], src[:, sh:], src[:, 0:E - sh], ALU.add))
                src, dst = dst, (ends2 if dst is ends else ends)
            ends = src
            own.step(dve, dve.tensor_tensor(base, ends, tiles, ALU.subtract))
            own.step(dve, dve.tensor_scalar(base, base, float(P), None, ALU.mult))
            own.step(dve, dve.tensor_tensor(eq, upto, of_tile, ALU.subtract))
            own.step(dve, dve.tensor_tensor(eq, eq, in_tile, ALU.add))
            own.step(dve, dve.tensor_tensor(eq, eq, base.unsqueeze(1).broadcast_to([P, NT, E]), ALU.add))
            own.step(dve, dve.tensor_tensor(eq, eq, oh, ALU.mult))
            own.step(dve, dve.tensor_reduce(rt[:, 3, :], eq, AX_X, ALU.add))
            dve.tensor_copy(slot[:, :], rt[:, 3, :]).then_inc(route_ready, 1)
            own.step(dve, dve.tensor_scalar(ids_f[:, :], tile_no[:, :], ends[:, 0:1], None, ALU.is_ge))
            for e in range(1, E - 1):
                own.step(dve, dve.scalar_tensor_tensor(out=ids_f[:, :], in0=tile_no[:, :], scalar=ends[:, e:e + 1],
                                                       in1=ids_f[:, :], op0=ALU.is_ge, op1=ALU.add))
            dve.tensor_copy(ids[:, :], ids_f[:, :]).then_inc(route_ready, 1)
            dve.wait_ge(emx_ready, 1)
            own.step(dve, dve.tensor_scalar(rt[:, 4, :], emx, 1.0, None, ALU.add))
            own.step(dve, dve.reciprocal(alpha[:, :], rt[:, 4, :]))
            dve.wait_ge(b1_ps, 1)
            w1v = W1s.rearrange("p (e c) -> p e c", e=E)
            dve.tensor_tensor(w1v[:, :, F:], out_ps[:, 0:E * FC].rearrange("p (e c) -> p e c", e=E),
                      b1T.rearrange("p (e c) -> p e c", e=E), ALU.add).then_inc(w1_ready, 1)

            def view(t):
                return t.rearrange("p (g r h) -> p g r h", g=H, h=H)

            def keys(t):
                return t.rearrange("p r g -> p g r").unsqueeze(3).broadcast_to([P, H, HP, H])

            def queries(t):
                return t.unsqueeze(1).broadcast_to([P, H, HP, H])

            def scores_of(n, q):
                m, p0 = (q // 2) % 2, HP * (q % 2)
                if q % 2 == 0:
                    dve.wait_ge(ready["qkvw"], n * 2 + 4)
                if not (isinstance(n, int) and n == 0):
                    dve.wait_ge(exp_ready, n)
                for d, dst in ((0, A), (1, Bb)):
                    ins = dve.tensor_tensor(view(dst[:, :]), queries(QK[:, m, d, 0, p0:p0 + HP, :]),
                                            keys(QK[:, m, d, 1, p0:p0 + HP, :]), ALU.mult)
                own.step(dve, ins)
                own.step(dve, dve.tensor_tensor(A[:, :], A[:, :], Bb[:, :], ALU.add))
                half, src = SZ // 2, A
                while half >= N:
                    own.step(dve, dve.tensor_tensor(Bb[:, 0:half], src[:, 0:half], src[:, half:2 * half], ALU.max))
                    half, src = half // 2, Bb
                dve.tensor_tensor(A[:, :].rearrange("p (g n) -> p g n", g=H), A[:, :].rearrange("p (g n) -> p g n", g=H),
                                  Bb[:, 0:N].unsqueeze(1).broadcast_to([P, H, N]), ALU.subtract).then_inc(s_ready, 1)

            def ev0(n, q, fold=False):
                m, p0 = q // 2, HP * (q % 2)
                if q % 2 == 0:
                    dve.wait_ge(vw_ready, n * 2 + 4)
                dve.wait_ge(exp_ready, n + 1)
                if not (isinstance(n, int) and n < 2):
                    dve.wait_ge(sum_ready, n - 1)
                ins = dve.tensor_tensor(view(EXY[:, q % 2, 1, :]), view(EXY[:, q % 2, 0, :]),
                                        keys(VW[:, m, 0, 0, p0:p0 + HP, :]), ALU.mult)
                if fold:
                    own.step(dve, ins)
                    dve.wait_ge(ev1_ready, n + 1)
                    lo, hi = EXY[:, q % 2, 0:2, 0:SZ // 2], EXY[:, q % 2, 0:2, SZ // 2:]
                    ins = dve.tensor_tensor(lo, lo, hi, ALU.add)
                ins.then_inc(ev0_ready, 1)

            def finish(bg, q):
                n = bg * NQ + q
                i, p0 = q // 2, HP * (q % 2)
                dve.wait_ge(sum_ready, n + 1)
                bank_ = sums[q % 2]
                own.step(dve, dve.reciprocal(rden[:, :], bank_[:, 0:N]))
                own.step(dve, dve.tensor_tensor(osb[:, :, :], bank_[:, N:3 * N].rearrange("p (d n) -> p d n", d=2),
                                                rden[:, :].unsqueeze(1).broadcast_to([P, 2, N]), ALU.mult))
                if q == 0 and not isinstance(bg, int) or q == 0 and bg:
                    dve.wait_ge(filled["oT"], bg * 4)
                dst = O[:, :, i * C + 2 * p0:i * C + 2 * p0 + 2 * HP].rearrange("p h (r d) -> p d r h", d=2)
                dve.tensor_tensor(dst, osb[:, :, :].rearrange("p d (r h) -> p d r h", h=H),
                                  VW[:, i, :, 1, p0:p0 + HP, :], ALU.mult).then_inc(f_ready, 1)

            dve.wait_ge(zeroed, 16 * ZERO_DMAS)
            scores_of(0, 0)
            scores_of(1, 1)
            ev0(0, 0)

            def body(bg, turn):
                last = turn is None and bg == NBG - 1
                for q in range(NQ):
                    if not last or q < NQ - 2:
                        scores_of(bg * NQ + q + 2, (q + 2) % NQ)
                    if not last or q < NQ - 1:
                        ev0(bg * NQ + q + 1, (q + 1) % NQ, turn is not None)
                    finish(bg, q)

            body(0, None)
            with dve.Fori(0, len(FFN_BGS)) as turn:
                own.turn(turn, NQ * 9)
                body(turn + FFN_BGS[0], turn)
            own.left(len(FFN_BGS))
            body(NBG - 1, None)

            def gate_in(bg, i):
                w = bg * NI + i
                dve.wait_ge(fx_in[i], (bg + 1) * 16)
                for k in range(2):
                    t = bg * 4 + i * BGT + k
                    ins = dve.tensor_scalar(fin_n[i][:, k * D:(k + 1) * D], fin_x[i][:, k * D:(k + 1) * D],
                                            RS[:, bass.ds(t, 1)], NM[:, bass.ds(t, 1)], ALU.mult, ALU.add)
                own.step(dve, ins)
                dve.wait_ge(fxn_ready, w + 1)
                for k in range(4):
                    t = bg * 4 + i * BGT + k
                    ins = dve.scalar_tensor_tensor(
                        out=fin_z[i][:, k * D:(k + 1) * D], in0=f_all[:, bass.ds(t * D, D)],
                        scalar=alpha[:, bass.ds(t, 1)], in1=fin_n[i][:, k * D:(k + 1) * D],
                        op0=ALU.mult, op1=ALU.add)
                ins.then_inc(z_ready, 1)

            def gated(bg, i):
                w = bg * NI + i
                dve.wait_ge(sg_ready, w + 1)
                dve.tensor_tensor(fin_z[i], fin_z[i], s_all[:, bass.ds(w * NF, NF)], ALU.mult).then_inc(g_ready, 1)

            dve.wait_ge(gathered[0], 16 * BGT)
            gate_in(0, 0)
            dve.wait_ge(gathered[1], 16 * (NT - BGT))
            dve.wait_ge(proj_ready, NBG * NI + 1)
            with dve.Fori(0, NBG - 1) as bg:
                own.turn(bg, NI)
                for i in range(NI):
                    if (i + 1) // NI:
                        dve.wait_ge(res_ready, bg * NI + 1)
                    gate_in(bg + (i + 1) // NI, (i + 1) % NI)
                    gated(bg, i)
            own.left(NBG - 1)
            for i in range(NI):
                if i + 1 < NI:
                    gate_in(NBG - 1, i + 1)
                gated(NBG - 1, i)


INS = ['L0_attn_x', 'L0_attn_w_qkvw', 'L0_attn_w_out', 'L0_ffn_centroids', 'L0_ffn_gamma', 'L0_ffn_beta',
       'L0_ffn_W1', 'L0_ffn_b1', 'L0_ffn_W2', 'L0_ffn_b2']


def kernel(**inputs):
    import numpy as np
    import concourse.bacc as bacc
    from concourse.bass_utils import run_bass_kernel_spmd

    nc = bacc.Bacc("TRN2", target_bir_lowering=False, num_devices=1)
    arrays, args = {}, []
    for name in INS:
        a = np.ascontiguousarray(inputs[name])
        arrays[f"in_{name}"] = a
        args.append(nc.dram_tensor(f"in_{name}", a.shape, mybir.dt.from_np(a.dtype), kind="ExternalInput").ap())
    out = nc.dram_tensor("out", inputs["L0_attn_x"].shape, F32, kind="ExternalOutput").ap()
    program(nc, *args, out)
    r = run_bass_kernel_spmd(nc, [arrays], core_ids=[0])
    return r.results[0]["out"]
```

```python
from contextlib import ExitStack

import concourse.bass as bass
from concourse import mybir

F32 = mybir.dt.float32
BF16 = mybir.dt.bfloat16
I32 = mybir.dt.int32
U32 = mybir.dt.uint32
ALU = mybir.AluOpType
ACT = mybir.ActivationFunctionType
AX_X = mybir.AxisListType.X

P = 128
D = 128
B, S = 32, 256
NT = B * S // P
H = 16
NI = 4
NR = 4
C = D // NI
NP = C // 2
SCALE = 2.0 ** -0.5
EPS = 1e-5

E = 8
F = 512
FC = F // P
FT = 72
FTL = FT + 4
NW1 = 3
W1C = F + FC

GT = 8
NG = NT // GT

NBG = 4
BGT = NT // NBG
HP = NP // 2
N = HP * H
SZ = H * N
NQ = 2 * NI
LOOP_BGS = (1, 2)
FFN_FIRST = [0] * 4 + [3] * 4
FFN_LOOP = [4, 4, 4, 3] * 2
PER_BG = sum(FFN_LOOP)
assert sum(FFN_FIRST) + PER_BG * len(LOOP_BGS) == FT
FOLD_FIRST, FOLD_LOOP, FOLD_LAST = [0] * 4 + [1] * 4, [1, 2] * 4, [0] * (NQ - 3) + [2] * 3
PROJECT_AT = ((1, 2), (1, 3), (2, 0), (2, 1))
START_EXPERTS = (3, 1)
EXP_BEHIND, SUM_BEHIND = 1, 3
ZERO_DMAS = -(-FTL * D // SZ)


class Count:

    def __init__(self, sem):
        self.sem, self.n, self.base = sem, 0, 0

    def inc(self, ins):
        ins.then_inc(self.sem, 1)
        self.n += 1

    def wait(self, eng):
        eng.wait_ge(self.sem, self.base + self.n)

    def step(self, eng, ins):
        self.inc(ins)
        self.wait(eng)

    def turn(self, it, per):
        self.start, self.per, self.base = self.n, per, it * per

    def left(self, turns):
        assert self.n - self.start == self.per, (self.n - self.start, self.per)
        self.n, self.base = self.start + turns * self.per, 0


def work_uses(bg, last):
    uses = []
    for q in range(NQ):
        m = q // 2
        if q == 4 and not last:
            uses += [(q, "xT", bg + 1, j) for j in range(4)]
        if q % 2 == 1 and (m < 2 or not last):
            uses += [(q, "qkvw", bg * NI + m + 2, j) for j in range(4)]
    return uses + [(NQ, "oT", bg, j) for j in range(4)]


def program(nc, x, w_qkvw, w_out, centroids, gamma, beta, W1, b1, W2, b2, out):
    with ExitStack() as ctx:
        def sb(name, shape, dt=F32):
            return ctx.enter_context(nc.sbuf_tensor(name, shape, dt))

        def sem(name):
            return ctx.enter_context(nc.semaphore(name))

        xs_dram = nc.dram_tensor("xs_dram", [FTL * P, D], F32, kind="Internal").ap()
        y_dram = nc.dram_tensor("y_dram", [FT * P, D], F32, kind="Internal").ap()

        xf = x.rearrange("b s d -> (b s) d")
        outf = out.rearrange("b s d -> (b s) d")

        A = sb("A", [P, SZ])
        Bb = sb("Bb", [P, SZ])
        EXY = sb("EXY", [P, 2, 3, SZ])
        QK = sb("QK", [P, 2, 2, 2, NP, H])
        VW = sb("VW", [P, NI, 2, 2, NP, H])
        x_bg = sb("x_bg", [P, BGT, D])
        xnT = sb("xnT", [P, BGT * P])
        OO = sb("OO", [P, 2 * H * D])
        OJ = x_bg[:, :, :].rearrange("p (i k) d -> p i (k d)", i=NI)
        O = OO[:, 0:H * D].rearrange("p (h c) -> p h c", h=H)
        OT = OO[:, H * D:]
        xhat = sb("xhat", [P, NT * D])
        s_all = xhat
        WW = sb("WW", [P, E * W1C + E * F])
        W1s = WW[:, 0:E * W1C]
        W2s = WW[:, E * W1C:]
        f_all = WW[:, 0:NT * D]
        w1slot = sb("w1slot", [P, NW1, W1C])
        xs = sb("xs", [P, 2, D])
        xsT = sb("xsT", [P, 2, P])
        hT = sb("hT", [P, 2, FC, P])
        ysb = sb("ysb", [P, 2, D])
        wq = sb("wq", [P, NI * NR * C])
        wo = sb("wo", [P, D])
        ident = sb("ident", [P, P])
        perm = sb("perm", [P, P])
        tri, onesb = OO[:, 3776:3840].bitcast(BF16), OO[:, 3840:3904].bitcast(BF16)
        row0 = sb("row0", [P, P])
        eps = sb("eps", [P, 1])
        b2row = sb("b2row", [P, E * D])
        small = OO[0:3 * E + E * FC, 3136:3136 + D]
        smallT = OO[:, 3904:3904 + 3 * E + E * FC]
        cT, gT, bT = (smallT[:, E * n:E * n + E] for n in range(3))
        b1T = smallT[:, 3 * E:]
        RS = sb("RS", [P, NT])
        NM = sb("NM", [P, NT])
        alpha = sb("alpha", [P, NT])
        slot = sb("slot", [P, NT], U32)
        ids = sb("ids", [P, FTL], I32)
        rden = sb("rden", [P, N])
        idle = sb("idle", [P, 1])
        osb = Bb[:, SZ - 2 * N:].rearrange("p (d n) -> p d n", d=2)
        tot_i = sb("tot_i", [P, E], I32)
        tile_no, ids_f = OO[:, 3264:3264 + FTL], OO[:, 3392:3392 + FTL]

        flat = EXY[:, :, :, :].rearrange("p a b n -> p (a b n)")
        G = GT * D
        x_st = flat[:, 0:NT * D]
        xn_st = [v.rearrange("p (k d) -> p k d", k=GT) for v in (A[:, 0:G], A[:, G:2 * G], flat[:, NT * D:NT * D + G])]
        xnT_g = QK[:, :, :, :, :, :].rearrange("p a b c r h -> p (a b c r h)")[:, 0:GT * P]
        zeros = Bb
        scores = OO[:, 0:512].rearrange("p (t e) -> p t e", e=E)
        eq = OO[:, 512:1024].rearrange("p (t e) -> p t e", e=E)
        oh = OO[:, 1024:1536].rearrange("p (t e) -> p t e", e=E)
        cum = [OO[:, 1536 + 512 * n:2048 + 512 * n].rearrange("p (t e) -> p t e", e=E) for n in range(2)]
        rt = OO[:, 2560:2560 + 5 * NT].rearrange("p (n t) -> p n t", n=5)
        ohb = OO[:, 2880:3136].bitcast(BF16)
        st = OO[:, 3472:3472 + 6 * GT].rearrange("p (k n) -> p k n", n=6)
        mv = OO[:, 3520:3520 + 6 * GT].rearrange("p (s k n) -> p s k n", s=3, n=2)
        dev, rs, nm, sq, dev2, rs2 = (OO[:, c:c + 3 * GT].rearrange("p (s k) -> p s k", s=3)
                                      for c in range(3568, 3568 + 18 * GT, 3 * GT))
        r8 = OO[:, 3712:3712 + 8 * E].rearrange("p (n e) -> p n e", e=E)

        bank = [ctx.enter_context(nc.psum_tensor(f"bank{n}", [P, 512], F32)) for n in range(8)]
        work = bank[0:2]
        sums = bank[2:4]
        hT_ps, xsT_ps, y_ps, out_ps = last_ps = bank[4:8]

        small_in, w_in, wraw_in = sem("small_in"), sem("w_in"), sem("wraw_in")
        x_in = [sem(f"x_in{n}") for n in range(3)]
        zeroed, scattered = sem("zeroed"), sem("scattered")
        gathered = [sem("gathered_first"), sem("gathered_rest")]
        consts, dve_own = sem("consts"), sem("dve_own")
        pool_own = sem("pool_own")
        smallT_ps, smallT_ready = sem("smallT_ps"), sem("smallT_ready")
        var1, dev1, var2, dev_2 = sem("var1_ready"), sem("dev1_ready"), sem("var2_ready"), sem("dev2_ready")
        rs2_ready = sem("rs2_ready")
        xn_ready, xnT_ps, xnT_sb = sem("xn_ready"), sem("xnT_ps"), sem("xnT_sb")
        sc_ps, sc_ready = sem("sc_ps"), sem("sc_ready")
        oh_ready, prefix_ps, mx_ready, emx_ready = sem("oh_ready"), sem("prefix_ps"), sem("mx_ready"), sem("emx_ready")
        route_ready, xhat_ready = sem("route_ready"), sem("xhat_ready")
        wT_ps, wT_ready, b1_ps, w1_ready = sem("wT_ps"), sem("wT_ready"), sem("b1_ps"), sem("w1_ready")
        xbg_in, xnb_ready = sem("xbg_in"), sem("xnb_ready")
        filled = {k: sem(k + "_ps") for k in ("qkvw", "xT", "oT")}
        ready = {k: sem(k + "_ready") for k in ("qkvw", "xT", "oT")}
        vw_ready = sem("vw_ready")
        s_ready, exp_ready = sem("s_ready"), sem("exp_ready")
        ev_ready = sem("ev_ready")
        sum_ready, f_ready = sem("sum_ready"), sem("f_ready")
        proj_ps, proj_ready, oj_in = sem("proj_ps"), sem("proj_ready"), sem("oj_in")
        xs_in = [sem("xs_in0"), sem("xs_in1")]
        w1_in = [sem(f"w1_in{n}") for n in range(NW1)]
        y_out = [sem("y_out0"), sem("y_out1")]
        xsT_full, xsT_ready = sem("xsT_full"), sem("xsT_ready")
        h_full, h_ready = sem("h_full"), sem("h_ready")
        y_full, y_ready = sem("y_full"), sem("y_ready")
        fx_in = [sem(f"fx_in{i}") for i in range(NI)]
        sg_ready = sem("sg_ready")
        fxn_ready, z_ready, res_ready = sem("fxn_ready"), sem("z_ready"), sem("res_ready")
        res_out = [sem(f"res_out{i}") for i in range(NI)]

        block = ctx.enter_context(nc.Block())

        def bgs(eng, body):
            body(0, None)
            with eng.Fori(0, len(LOOP_BGS)) as turn:
                body(turn + LOOP_BGS[0], turn)
            body(NBG - 1, None)

        def groups(eng, step):
            step(0, 0, 0)
            with eng.Fori(0, (NG - 2) // 3) as it:
                for j in range(1, 4):
                    step(it * 3 + j, j % 3, it + j // 3)
            step(NG - 1, (NG - 1) % 3, (NG - 1) // 3)

        def ffn_tiles(bg, turn):
            if turn is None and bg == NBG - 1:
                return [[]] * NQ
            k, at = (0, 0) if turn is None else (sum(FFN_FIRST), turn * PER_BG)
            steps = []
            for n in FFN_FIRST if turn is None else FFN_LOOP:
                steps.append([(at + k + j, k + j, 0 if turn is None else turn) for j in range(n)])
                k += n
            return steps

        def folds(bg, turn):
            return FOLD_LOOP if turn is not None else FOLD_FIRST if bg == 0 else FOLD_LAST

        def nth_use(j, turn, slots):
            return turn * (PER_BG // slots) + j // slots + 1

        NF = 4 * D
        qk_flat = QK[:, :, :, :, :, :].rearrange("p a b c r h -> p (a b c r h)")
        fin_x, fin_z, fin_n, fin_r = ([buf[:, i * NF:(i + 1) * NF] for i in range(NI)] for buf in (xnT, A, Bb, qk_flat))

        def fin_rows(ap, bg, i):
            t0 = i * BGT + bg * 4
            return ap[bass.ds(t0 * P, NF // D * P), :].rearrange("(k p) d -> p k d", p=P)

        @block.sync
        def _(sp):
            for g in range(NG):
                if g >= 3:
                    sp.wait_ge(x_in[g % 3], g // 3 * 16)
                sp.dma_start(x_st[:, g * G:(g + 1) * G].rearrange("p (k d) -> p k d", k=GT),
                             xf[g * GT * P:(g + 1) * GT * P, :].rearrange("(k p) d -> p k d", p=P))\
                    .then_inc(x_in[g % 3], 16)
            sp.dma_start(wq[:, :], w_qkvw).then_inc(w_in, 16)
            sp.dma_start(wo[:, :], w_out).then_inc(w_in, 16)
            sp.wait_ge(consts, 7)
            sp.dma_start(b2row[0:1, :], b2.rearrange("(a e) d -> a (e d)", a=1)).then_inc(w_in, 16)

            def load_bg(bg):
                for k in range(0, BGT, GT):
                    sp.dma_start(x_bg[:, k:k + GT, :], xf[bass.ds(bg * (BGT * P) + k * P, GT * P), :]
                                 .rearrange("(k p) d -> p k d", p=P)).then_inc(xbg_in, 16)

            load_bg(0)
            for e in range(E):
                sp.dma_start(W1s[:, e * W1C:e * W1C + F].rearrange("p (c d) -> p c d", d=D),
                             W1[e, :, :].rearrange("(c p) d -> p c d", p=P)).then_inc(wraw_in, 16)
            sp.dma_start(W2s.rearrange("p (e f) -> p e f", f=F), W2.rearrange("e n f -> n e f")).then_inc(wraw_in, 16)

            def load_xs(k, j):
                sp.dma_start(xs[:, j % 2, :], xs_dram[bass.ds(k * P, P), :]).then_inc(xs_in[j % 2], 16)

            def load_w1(k, j):
                e = sp.value_load(ids[0:1, bass.ds(k, 1)], min_val=0, max_val=E - 1)
                sp.dma_start(w1slot[:, j % NW1, :], W1s[:, bass.ds(e * W1C, W1C)]).then_inc(w1_in[j % NW1], 16)

            for s in range(2):
                sp.sem_inc(y_out[s], 16)
            for i in range(NI):
                sp.sem_inc(res_out[i], 16)

            def body(bg, turn):
                if turn is None and bg == NBG - 1:
                    return
                if turn is None:
                    sp.wait_ge(filled["xT"], 4)
                    load_bg(1)
                    sp.wait_ge(route_ready, 2)
                    sp.wait_ge(w1_ready, 2)
                    sp.wait_ge(scattered, 16 * NT)
                    for k in range(2):
                        load_xs(k, k)
                        load_w1(k, k)
                    load_w1(2, 2)
                    for k in range(2, 4):
                        sp.wait_ge(xsT_full, k - 1)
                        load_xs(k, k)
                    sp.wait_ge(h_ready, FC)
                    load_w1(3, 3)
                for q, steps in enumerate(ffn_tiles(bg, turn)):
                    if q == 3 and turn is not None:
                        sp.wait_ge(proj_ps, bg * NI)
                        load_bg(bg + 1)
                    for k, j, _ in steps:
                        sp.wait_ge(xsT_full, k + 3)
                        load_xs(k + 4, j + 4)
                        sp.wait_ge(h_ready, (k + 2) * FC)
                        load_w1(k + 4, j + 4)
                        sp.wait_ge(y_ready, k + 2)
                        sp.dma_start(y_dram[bass.ds(k * P, P), :], ysb[:, j % 2, :]).then_inc(y_out[j % 2], 16)

            bgs(sp, body)

            def load_fin(bg, i):
                sp.dma_start(fin_x[i].rearrange("p (k d) -> p k d", d=D), fin_rows(xf, bg, i)).then_inc(fx_in[i], 16)

            def store_fin(bg, i):
                sp.wait_ge(res_ready, bg * NI + i + 1)
                sp.dma_start(fin_rows(outf, bg, i), fin_r[i].rearrange("p (k d) -> p k d", d=D))\
                    .then_inc(res_out[i], 16)

            sp.wait_ge(filled["qkvw"], NBG * NI * 4)
            for i in range(NI):
                load_fin(0, i)
            with sp.Fori(0, NBG - 1) as bg:
                for i in range(NI):
                    store_fin(bg, i)
                    load_fin(bg + 1, i)
            for i in range(NI):
                store_fin(NBG - 1, i)
            for i in range(NI):
                sp.wait_ge(res_out[i], 16 * (1 + NBG))

        @block.gpsimd
        def _(pool):
            own = Count(pool_own)
            own.inc(pool.memset(ident[:, :], 0.0))
            own.inc(pool.memset(tri[:, :], 1.0))
            pool.memset(onesb[:, :], 1.0).then_inc(consts, 1)
            own.inc(pool.memset(row0[:, :], 0.0))
            own.inc(pool.memset(b2row[:, :], 0.0))
            pool.memset(eps[:, :], EPS).then_inc(consts, 1)
            own.wait(pool)
            pool.affine_select(out=ident[:, :], in_=ident[:, :], compare_op=ALU.not_equal, fill=1.0, base=0,
                               pattern=[[-1, P]], channel_multiplier=1).then_inc(consts, 1)
            pool.memset(row0[0:1, :], 1.0).then_inc(consts, 1)
            pool.wait_ge(consts, 4)
            pool.tensor_copy(perm[:, :].rearrange("p (j m) -> p j m", j=4),
                             ident[:, :].rearrange("p (m j) -> p j m", j=4)).then_inc(consts, 1)
            pool.affine_select(out=tri[:, :], in_=tri[:, :], compare_op=ALU.is_gt, fill=0.0, base=0,
                               pattern=[[1, P]], channel_multiplier=-1).then_inc(consts, 1)
            pool.iota(tile_no[:, :], [[1, FTL]], base=0, channel_multiplier=0,
                      allow_small_or_imprecise_dtypes=True).then_inc(consts, 1)
            own.step(pool, pool.memset(zeros[:, :], 0.0))
            pool.wait_ge(xn_ready, 4)
            flat_xs = xs_dram.rearrange("(p r) d -> p (r d)", p=P)
            per, at = FTL * D, 0
            while at < per:
                n = min(SZ, per - at)
                pool.dma_start(flat_xs[:, at:at + n], zeros[:, 0:n]).then_inc(zeroed, 16)
                at += n
            pool.wait_ge(zeroed, 16 * ZERO_DMAS)

            def scatter(t):
                pool.indirect_dma_start(out=xs_dram, out_offset=bass.IndirectOffsetOnAxis(ap=slot[:, t:t + 1], axis=0),
                                        in_=xhat[:, t * D:(t + 1) * D], in_offset=None).then_inc(scattered, 16)

            pool.wait_ge(route_ready, 1)
            pool.wait_ge(xhat_ready, NG)
            for t in range(NT):
                scatter(t)

            def swap(bg):
                pool.wait_ge(ready["oT"], bg * 4 + 4)
                if bg < NBG - 1:
                    pool.wait_ge(filled["xT"], (bg + 2) * 4)
                if bg:
                    pool.wait_ge(proj_ps, bg * NI)
                for i in range(NI):
                    for j in range(4):
                        pool.dma_start(OJ[C * j:C * j + C, i, :], OT[C * i:C * i + C, 4 * P * j:4 * P * (j + 1)])\
                            .then_inc(oj_in, 16)

            for bg in range(NBG - 1):
                swap(bg)

            for s in range(2):
                pool.wait_ge(y_out[s], 16 * (1 + FT // 2))
            pool.wait_ge(h_full, FT + 1)
            for s in range(NW1):
                pool.wait_ge(w1_in[s], 16 * (FT // NW1 + (4 + NW1 - 1 - s) // NW1))
            order = [i * BGT + b * 4 + k for b in range(NBG) for i in range(NI) for k in range(4)]
            for m, t in enumerate(order):
                pool.indirect_dma_start(out=f_all[:, t * D:(t + 1) * D], out_offset=None, in_=y_dram,
                                        in_offset=bass.IndirectOffsetOnAxis(ap=slot[:, t:t + 1], axis=0))\
                    .then_inc(gathered[m >= BGT], 16)
            swap(NBG - 1)

        @block.scalar
        def _(act):
            for n, w in enumerate((centroids, gamma, beta)):
                act.dma_start(small[E * n:E * n + E, :], w).then_inc(small_in, 16)
            act.dma_start(small[3 * E:, :], b1.rearrange("e (c f) -> (e c) f", c=FC)).then_inc(small_in, 16)
            act.wait_ge(smallT_ps, 1)
            act.activation(smallT[:, :], work[0][:, 0:3 * E + E * FC], ACT.Copy).then_inc(smallT_ready, 1)

            act.wait_ge(consts, 7)

            def deviation(g, s):
                act.wait_ge(var1, g + 1)
                act.activation(dev[:, s, :], mv[:, s, :, 1], ACT.Sqrt, bias=eps[:, 0:1]).then_inc(dev1, 1)

            def copy_scores(g):
                act.wait_ge(sc_ps, g + 1)
                act.activation(scores[:, bass.ds(g * GT, GT), :].rearrange("p t e -> p (t e)"), out_ps[:, 0:GT * E],
                               ACT.Copy).then_inc(sc_ready, 1)

            def second_norm(g, s):
                act.wait_ge(rs2_ready, g + 1)
                for k in range(GT):
                    ins = act.activation(xhat[:, bass.ds(g * (GT * D) + k * D, D)], xn_st[s][:, k, :], ACT.Copy,
                                         scale=rs2[:, s, k:k + 1])
                ins.then_inc(xhat_ready, 1)

            def group(g, s, first=False):
                act.wait_ge(var2, g + 1)
                act.activation(dev2[:, s, :], sq[:, s, :], ACT.Sqrt, bias=eps[:, 0:1]).then_inc(dev_2, 1)
                if not first:
                    second_norm(g - 1, (s - 1) % 3)
                    copy_scores(g - 1)
                for j in range(2):
                    act.wait_ge(xnT_ps, g * 2 + j + 1)
                    if j == 0 and not first:
                        act.wait_ge(sc_ps, g)
                    act.activation(xnT_g[:, 512 * j:512 * j + 512], work[j][:, :], ACT.Copy).then_inc(xnT_sb, 1)
            deviation(0, 0)
            deviation(1, 1)
            group(0, 0, True)
            with act.Fori(0, (NG - 2) // 3) as it:
                for j in range(1, 4):
                    g = it * 3 + j
                    deviation(g + 1, (j + 1) % 3)
                    group(g, j % 3)
            group(NG - 1, (NG - 1) % 3)
            second_norm(NG - 1, (NG - 1) % 3)
            copy_scores(NG - 1)
            act.wait_ge(mx_ready, 1)
            act.activation(rt[:, 2, :], rt[:, 0, :], ACT.Exp, scale=-1.0).then_inc(emx_ready, 1)

            def evac_w(u):
                act.wait_ge(wT_ps, u + 1)
                e = u % E
                dst = W1s[:, e * W1C:e * W1C + F] if u < E else W2s[:, e * F:(e + 1) * F]
                act.activation(dst, work[u % 2][:, :], ACT.Copy).then_inc(wT_ready, 1)

            def fin_norm(bg, i):
                act.wait_ge(fx_in[i], (bg + 1) * 16)
                for k in range(4):
                    t = bg * 4 + i * BGT + k
                    ins = act.activation(fin_n[i][:, k * D:(k + 1) * D], fin_x[i][:, k * D:(k + 1) * D],
                                         ACT.Identity, scale=RS[:, bass.ds(t, 1)], bias=NM[:, bass.ds(t, 1)])
                ins.then_inc(fxn_ready, 1)

            def normalise(bg):
                act.wait_ge(xbg_in, (bg + 1) * (16 * BGT // GT))
                for k in range(BGT):
                    t = bg * BGT + k
                    ins = act.activation(x_bg[:, k, :], x_bg[:, k, :], ACT.Identity, scale=RS[:, bass.ds(t, 1)],
                                         bias=NM[:, bass.ds(t, 1)])
                ins.then_inc(xnb_ready, 1)

            def evac(kind, n, j, u):
                act.wait_ge(filled[kind], n * 4 + j + 1)
                src = work[u % 2]
                if kind == "xT":
                    if not isinstance(n, int) or n:
                        act.wait_ge(filled["qkvw"], n * 4 * NI)
                    tok = xnT[:, :].rearrange("p (h b a) -> p b h a", h=H, a=H)
                    dst = tok[:, 2 * j:2 * j + 2, :, :]
                    src = src[:, :].rearrange("p (b h a) -> p b h a", b=2, h=H)
                elif kind == "oT":
                    if not isinstance(n, int) or n:
                        act.wait_ge(oj_in, n * (16 * NI * 4))
                    dst = OT.rearrange("p (m h a) -> p h m a", h=H, a=4)[:, 4 * j:4 * j + 4, :, :]
                    src = src[:, :].rearrange("p (h m a) -> p h m a", h=4, a=4)
                else:
                    i = evac.i
                    if not isinstance(n, int) or n >= 2:
                        act.wait_ge(s_ready, n * 2 - 2)
                    if not isinstance(n, int) or n >= NI:
                        act.wait_ge(f_ready, n * 2 - 6)
                    hh = H // 4
                    src = src[:, :].rearrange("p (h rc d) -> p d rc h", h=hh, d=2)
                    dst = VW[:, i, :, :, :, hh * j:hh * j + hh].rearrange("p d r c h -> p d (r c) h")
                    act.activation(dst, src[:, :, 2 * NP:, :], ACT.Copy).then_inc(vw_ready, 1)
                    dst = QK[:, i % 2, :, :, :, hh * j:hh * j + hh].rearrange("p d r c h -> p d (r c) h")
                    src = src[:, :, 0:2 * NP, :]
                act.activation(dst, src, ACT.Copy).then_inc(ready[kind], 1)

            def exp(n, q):
                act.wait_ge(s_ready, n + 1)
                if not (isinstance(n, int) and n < 2):
                    act.wait_ge(sum_ready, n - 1)
                act.activation(EXY[:, q % 2, 0, :], A[:, :], ACT.Exp, scale=SCALE).then_inc(exp_ready, 1)

            def evac_xsT(k, j):
                act.wait_ge(xsT_full, k + 1)
                if not (isinstance(k, int) and k < 2):
                    act.wait_ge(h_full, k - 1)
                act.activation(xsT[:, j % 2, :], xsT_ps[:, 0:P], ACT.Copy).then_inc(xsT_ready, 1)

            def relu(k, j):
                act.wait_ge(h_full, k + 1)
                if not (isinstance(k, int) and k < 2):
                    act.wait_ge(y_full, k)
                for c in range(FC):
                    act.activation(hT[:, j % 2, c, :], hT_ps[:, c * P:(c + 1) * P], ACT.Relu,
                                   bias=w1slot[:, j % NW1, F + c:F + c + 1]).then_inc(h_ready, 1)

            def evac_y(k, j, turn):
                act.wait_ge(y_full, k + 2)
                act.wait_ge(y_out[j % 2], nth_use(j, turn, 2) * 16)
                act.activation(ysb[:, j % 2, :], y_ps[:, 0:D], ACT.Copy).then_inc(y_ready, 1)

            def ffn_tile(k, j, turn):
                evac_xsT(k + 2, j + 2)
                relu(k + 1, j + 1)
                evac_y(k, j, turn)

            act.sem_inc(y_ready, 1)
            act.sem_inc(proj_ready, 1)
            normalise(0)
            for j in range(4):
                evac("xT", 0, j, j)
            for c in range(2):
                for j in range(4):
                    evac.i = c
                    evac("qkvw", c, j, j)
            for u in range(E):
                evac_w(u)
            exp(0, 0)
            act.wait_ge(b1_ps, 1)
            for e in range(E):
                ins = act.activation(W1s[:, e * W1C:e * W1C + F], W1s[:, e * W1C:e * W1C + F], ACT.Copy,
                                     scale=gT[:, e:e + 1])
            ins.then_inc(w1_ready, 1)
            exp(1, 1)
            for u in range(E, 2 * E):
                evac_w(u)

            def evac_proj(bg, i):
                w = bg * NI + i
                act.wait_ge(scattered, 16 * NT)
                act.wait_ge(proj_ps, w + 1)
                act.activation(s_all[:, bass.ds(w * 512, 512)], out_ps[:, :], ACT.Copy).then_inc(proj_ready, 1)

            def body(bg, turn):
                first, last = turn is None and bg == 0, turn is None and bg == NBG - 1
                uses = work_uses(bg, last)
                ffn = ffn_tiles(bg, turn)
                for q in range(NQ + 1):
                    if last and q == NQ:
                        act.wait_ge(s_ready, NBG * NQ)
                        fin_norm(0, 0)
                        fin_norm(0, 1)
                    for u, (qq, kind, n, j) in enumerate(uses):
                        if qq == q:
                            evac.i = (q // 2 + 2) % NI
                            evac(kind, n, j, u)
                    if q == NQ:
                        break
                    for m in range(max(FFN_LOOP)):
                        if m < len(ffn[q]):
                            ffn_tile(*ffn[q][m])
                        if m == EXP_BEHIND and (not last or q < NQ - 2):
                            exp(bg * NQ + q + 2, q)
                        if first and (q, m) == START_EXPERTS:
                            evac_xsT(0, 0)
                            evac_xsT(1, 1)
                            relu(0, 0)
                        if (q, m) in PROJECT_AT and not first:
                            evac_proj(bg - 1, PROJECT_AT.index((q, m)))
                    if q == (1 if first else 3) and not last:
                        normalise(bg + 1)

            bgs(act, body)

            act.wait_ge(f_ready, NBG * NQ)

            def gate(bg, i):
                act.wait_ge(z_ready, bg * NI + i + 1)
                act.activation(fin_z[i], fin_z[i], ACT.Silu).then_inc(sg_ready, 1)

            with act.Fori(0, NBG - 1) as bg:
                for i in range(NI):
                    gate(bg, i)
                    fin_norm(bg + (i + 2) // NI, (i + 2) % NI)
            for i in range(NI):
                gate(NBG - 1, i)
                if i < 2:
                    fin_norm(NBG - 1, i + 2)

        @block.tensor
        def _(pe):
            pe.wait_ge(consts, 7)
            pe.wait_ge(small_in, 64)
            rows = 3 * E + E * FC
            pe.transpose(work[0][:, 0:rows], small[:, :], ident[0:rows, 0:rows]).then_inc(smallT_ps, 1)
            pe.wait_ge(smallT_ready, 1)

            def group(g, s, m):
                first = isinstance(g, int) and g == 0
                pe.wait_ge(xn_ready, g + 1)
                for j in range(2):
                    if not first:
                        pe.wait_ge(xnT_sb, g * 2 + j - 1)
                    for k in range(4):
                        ins = pe.transpose(work[j][:, k * P:(k + 1) * P], xn_st[s][:, 4 * j + k, :], ident[:, :])
                    ins.then_inc(xnT_ps, 1)
                if not first:
                    pe.wait_ge(sc_ready, g)
                for k in range(GT):
                    if k % 4 == 0:
                        pe.wait_ge(xnT_sb, g * 2 + k // 4 + 1)
                    ins = pe.matmul(out_ps[:, k * E:(k + 1) * E], xnT_g[:, k * P:(k + 1) * P], cT,
                                    start=True, stop=True)
                ins.then_inc(sc_ps, 1)

            groups(pe, group)
            pe.wait_ge(oh_ready, 1)
            pe.matmul(sums[0][:, :], tri[:, :], ohb[:, :], start=True, stop=True)
            pe.matmul(sums[1][:, :], onesb[:, :], ohb[:, :], start=True, stop=True).then_inc(prefix_ps, 1)

            def transpose_w(u):
                e = u % E
                if u >= 2:
                    pe.wait_ge(wT_ready, u - 1)
                for c in range(FC):
                    src = W1s[:, e * W1C + c * P:e * W1C + (c + 1) * P] if u < E else \
                        W2s[:, e * F + c * P:e * F + (c + 1) * P]
                    ins = pe.transpose(work[u % 2][:, c * P:(c + 1) * P], src, ident[:, :])
                ins.then_inc(wT_ps, 1)

            def fill(kind, n, j, u):
                dst = work[u % 2]
                if kind == "xT":
                    if j == 0:
                        pe.wait_ge(xnb_ready, n + 1)
                    for k in range(4):
                        ins = pe.transpose(dst[:, k * P:(k + 1) * P], x_bg[:, 4 * j + k, :], ident[:, :])
                elif kind == "oT":
                    if j == 0:
                        pe.wait_ge(f_ready, n * NQ + NQ)
                    for k in range(4):
                        ins = pe.transpose(dst[:, k * P:(k + 1) * P], O[:, 4 * j + k, :], perm[:, :])
                else:
                    hh, tok = H // 4, xnT[:, :].rearrange("p (h n) -> p h n", h=H)
                    for h in range(hh):
                        ins = pe.matmul(dst[:, h * NR * C:(h + 1) * NR * C], tok[:, hh * j + h, :],
                                        wq[:, fill.i * NR * C:(fill.i + 1) * NR * C], start=True, stop=True)
                ins.then_inc(filled[kind], 1)

            def copied(kind, n, j):
                pe.wait_ge(ready[kind], n * 4 + j + 1)

            def sum_keys(n, q, folded=0):
                pe.wait_ge(ev_ready, n + 1)
                if not (isinstance(n, int) and n < 2):
                    pe.wait_ge(f_ready, n - 1)
                for g in range(H):
                    parts = 3 - folded if g >= H // 2 else 3
                    ins = pe.matmul(sums[q % 2][:, 0:parts * N], ident[:, :], EXY[:, q % 2, 0:parts, g * N:(g + 1) * N],
                                    start=(g == 0), stop=(g == H - 1))
                ins.then_inc(sum_ready, 1)

            def ffn_transpose(k, j, turn):
                pe.wait_ge(xs_in[j % 2], nth_use(j, turn, 2) * 16)
                if not (isinstance(k, int) and k < 1):
                    pe.wait_ge(xsT_ready, k)
                pe.transpose(xsT_ps[:, 0:P], xs[:, j % 2, :], ident[:, :]).then_inc(xsT_full, 1)

            def ffn_up(k, j, turn):
                pe.wait_ge(w1_in[j % NW1], nth_use(j, turn, NW1) * 16)
                pe.wait_ge(xsT_ready, k + 1)
                if not (isinstance(k, int) and k < 1):
                    pe.wait_ge(h_ready, k * FC)
                for c in range(FC):
                    ins = pe.matmul(hT_ps[:, c * P:(c + 1) * P], w1slot[:, j % NW1, c * P:(c + 1) * P],
                                    xsT[:, j % 2, :], start=True, stop=True)
                ins.then_inc(h_full, 1)

            def ffn_down(k, j):
                e = pe.value_load(ids[0:1, bass.ds(k, 1)], min_val=0, max_val=E - 1)
                pe.wait_ge(y_ready, k + 1)
                pe.matmul(y_ps[:, 0:D], row0[:, :], b2row[:, bass.ds(e * D, D)], start=True, stop=False)
                pe.wait_ge(h_ready, (k + 1) * FC)
                for c in range(FC):
                    ins = pe.matmul(y_ps[:, 0:D], hT[:, j % 2, c, :], W2s[:, bass.ds(e * F + c * P, D)],
                                    start=False, stop=(c == FC - 1))
                ins.then_inc(y_full, 1)

            def ffn_tile(k, j, turn):
                ffn_transpose(k + 2, j + 2, turn)
                ffn_up(k + 1, j + 1, turn)
                ffn_down(k, j)

            pe.sem_inc(y_full, 1)
            pe.wait_ge(w_in, 16 * 3)
            pe.wait_ge(xnT_sb, 2 * NG)
            for j in range(4):
                if j >= 2:
                    copied("xT", 0, j - 2)
                fill("xT", 0, j, j)
            copied("xT", 0, 3)
            for c in range(2):
                for j in range(4):
                    if c or j >= 2:
                        copied("qkvw", (4 * c + j - 2) // 4, (j - 2) % 4)
                    fill.i = c
                    fill("qkvw", c, j, j)
            pe.wait_ge(wraw_in, 16 * (E + 1))
            copied("qkvw", 1, 3)
            for u in range(E):
                transpose_w(u)
            pe.wait_ge(sc_ready, NG)
            pe.wait_ge(wT_ready, E)
            for m in range(E * FC):
                e, c = m // FC, m % FC
                ins = pe.matmul(out_ps[:, m:m + 1], W1s[:, e * W1C + c * P:e * W1C + (c + 1) * P], bT[:, e:e + 1],
                                start=True, stop=True)
            ins.then_inc(b1_ps, 1)
            for u in range(E, 2 * E):
                transpose_w(u)
            sum_keys(0, 0)
            pe.wait_ge(wT_ready, 2 * E)

            def project(bg, i):
                w = bg * NI + i
                pe.wait_ge(w1_ready, 2)
                pe.wait_ge(oj_in, bg * (16 * NI * 4) + 16 * NI * 4)
                last = isinstance(bg, int) and bg == NBG - 1
                pe.wait_ge(proj_ready, (NBG - 1) * NI + 1 if last else w + 1)
                dst = last_ps[i] if last else out_ps
                for b in range(4):
                    ins = pe.matmul(dst[:, b * D:(b + 1) * D], OJ[:, i, b * P:(b + 1) * P], wo[:, :],
                                    start=True, stop=True)
                ins.then_inc(proj_ps, 1)

            def body(bg, turn):
                first, last = turn is None and bg == 0, turn is None and bg == NBG - 1
                uses = work_uses(bg, last)
                if isinstance(bg, int) and bg == 0:
                    before = [("qkvw", 1, 2), ("qkvw", 1, 3)]
                else:
                    before = [("oT", bg - 1, 2), ("oT", bg - 1, 3)]
                before += [(kind, n, j) for _, kind, n, j in uses]
                ffn, fold = ffn_tiles(bg, turn), folds(bg, turn)
                for q in range(NQ + 1):
                    for u, (qq, kind, n, j) in enumerate(uses):
                        if qq == q:
                            if kind == "qkvw":
                                fill.i = (q // 2 + 2) % NI
                                if fill.i == 0 and j == 0:
                                    pe.wait_ge(ready["xT"], bg * 4 + 8)
                            copied(*before[u])
                            fill(kind, n, j, u)
                    if q == NQ:
                        if last:
                            for i in range(NI):
                                project(bg, i)
                        break
                    for m in range(max(FFN_LOOP)):
                        if m < len(ffn[q]):
                            ffn_tile(*ffn[q][m])
                        if first and (q, m) == START_EXPERTS:
                            ffn_transpose(0, 0, 0)
                            ffn_transpose(1, 1, 0)
                            ffn_up(0, 0, 0)
                        if (q, m) in PROJECT_AT and not first:
                            project(bg - 1, PROJECT_AT.index((q, m)))
                        if m == SUM_BEHIND and (not last or q < NQ - 1):
                            sum_keys(bg * NQ + q + 1, q + 1, fold[q])

            bgs(pe, body)

        @block.vector
        def _(dve):
            own = Count(dve_own)

            def stats(g, s, m):
                if not (isinstance(g, int) and g == 0):
                    dve.wait_ge(var1, g)
                dve.wait_ge(x_in[s], (m + 1) * 16)
                for k in range(GT):
                    ins = dve.bn_stats(st[:, k, :], x_st[:, bass.ds(g * G + k * D, D)])
                own.step(dve, ins)
                dve.memset(idle[:, :], 0.0)
                for k in range(GT):
                    ins = dve.bn_aggr(mv[:, s, k, :], st[:, k, :])
                ins.then_inc(var1, 1)

            def norm(g, s, first=False):
                dve.wait_ge(dev1, g + 1)
                own.step(dve, dve.reciprocal(rs[:, s, :], dev[:, s, :]))
                own.inc(dve.scalar_tensor_tensor(out=nm[:, s, :], in0=mv[:, s, :, 0], scalar=-1.0, in1=rs[:, s, :],
                                                 op0=ALU.mult, op1=ALU.mult))
                own.step(dve, dve.tensor_tensor(sq[:, s, :], rs[:, s, :], rs[:, s, :], ALU.mult))
                dve.tensor_tensor(sq[:, s, :], sq[:, s, :], mv[:, s, :, 1], ALU.mult).then_inc(var2, 1)
                dve.tensor_copy(RS[:, bass.ds(g * GT, GT)], rs[:, s, :])
                dve.tensor_copy(NM[:, bass.ds(g * GT, GT)], nm[:, s, :])
                if not first:
                    dve.wait_ge(xnT_ps, g * 2 - 4)
                    dve.wait_ge(xhat_ready, g - 2)
                for k in range(GT):
                    ins = dve.tensor_scalar(xn_st[s][:, k, :], x_st[:, bass.ds(g * G + k * D, D)], rs[:, s, k:k + 1], nm[:, s, k:k + 1],
                                            ALU.mult, ALU.add)
                ins.then_inc(xn_ready, 1)

            def second_deviation(g, s):
                dve.wait_ge(dev_2, g + 1)
                dve.reciprocal(rs2[:, s, :], dev2[:, s, :]).then_inc(rs2_ready, 1)

            dve.wait_ge(consts, 7)
            stats(0, 0, 0)
            stats(1, 1, 0)
            norm(0, 0, True)
            stats(2, 2, 0)
            second_deviation(0, 0)
            norm(1, 1, True)
            stats(3, 0, 1)
            second_deviation(1, 1)
            norm(2, 2, True)
            with dve.Fori(1, (NG - 2) // 3) as it:
                own.turn(it - 1, 12)
                for j in range(1, 4):
                    stats(it * 3 + j, j % 3, it + j // 3)
                    second_deviation(it * 3 + j - 2, (j - 2) % 3)
                    norm(it * 3 + j - 1, (j - 1) % 3)
            own.left((NG - 2) // 3 - 1)
            stats(NG - 1, (NG - 1) % 3, (NG - 1) // 3)
            second_deviation(NG - 3, (NG - 3) % 3)
            norm(NG - 2, (NG - 2) % 3)
            second_deviation(NG - 2, (NG - 2) % 3)
            norm(NG - 1, (NG - 1) % 3)
            second_deviation(NG - 1, (NG - 1) % 3)

            dve.wait_ge(sc_ready, NG)
            mx, emx, taken = rt[:, 0, :], rt[:, 2, :], rt[:, 1, :]
            dve.tensor_reduce(mx, scores, AX_X, ALU.max).then_inc(mx_ready, 1)
            dve.wait_ge(mx_ready, 1)
            own.inc(dve.memset(taken, 0.0))
            own.step(dve, dve.tensor_tensor(eq, scores, mx.unsqueeze(2).broadcast_to([P, NT, E]), ALU.is_ge))
            for e in range(E):
                own.inc(dve.tensor_tensor(oh[:, :, e], eq[:, :, e], taken, ALU.is_gt))
                own.step(dve, dve.tensor_tensor(taken, taken, eq[:, :, e], ALU.max))
            dve.tensor_copy(ohb[:, :], oh.rearrange("p t e -> p (t e)")).then_inc(oh_ready, 1)
            dve.wait_ge(prefix_ps, 1)
            in_tile = sums[0][:, :].rearrange("p (t e) -> p t e", e=E)
            of_tile = sums[1][:, :].rearrange("p (t e) -> p t e", e=E)
            own.step(dve, dve.tensor_copy(cum[0], of_tile))
            shift, at = 1, 0
            while shift < NT:
                src, dst = cum[at], cum[1 - at]
                own.inc(dve.tensor_copy(dst[:, 0:shift, :], src[:, 0:shift, :]))
                own.step(dve, dve.tensor_tensor(dst[:, shift:, :], src[:, shift:, :], src[:, 0:NT - shift, :], ALU.add))
                shift, at = 2 * shift, 1 - at
            upto = cum[at]
            own.step(dve, dve.tensor_scalar(tot_i[:, :], upto[:, NT - 1, :], float(P - 1), None, ALU.add))
            own.step(dve, dve.tensor_scalar(tot_i[:, :], tot_i[:, :], P.bit_length() - 1, None, ALU.logical_shift_right))
            tiles, ends, ends2, base = (r8[:, n, :] for n in range(4))
            own.step(dve, dve.tensor_copy(tiles, tot_i[:, :]))
            src, dst = tiles, ends
            for sh in (1, 2, 4):
                own.inc(dve.tensor_copy(dst[:, 0:sh], src[:, 0:sh]))
                own.step(dve, dve.tensor_tensor(dst[:, sh:], src[:, sh:], src[:, 0:E - sh], ALU.add))
                src, dst = dst, (ends2 if dst is ends else ends)
            ends = src
            own.step(dve, dve.tensor_tensor(base, ends, tiles, ALU.subtract))
            own.step(dve, dve.tensor_scalar(base, base, float(P), None, ALU.mult))
            own.step(dve, dve.tensor_tensor(eq, upto, of_tile, ALU.subtract))
            own.step(dve, dve.tensor_tensor(eq, eq, in_tile, ALU.add))
            own.step(dve, dve.tensor_tensor(eq, eq, base.unsqueeze(1).broadcast_to([P, NT, E]), ALU.add))
            own.step(dve, dve.tensor_tensor(eq, eq, oh, ALU.mult))
            own.step(dve, dve.tensor_reduce(rt[:, 3, :], eq, AX_X, ALU.add))
            dve.tensor_copy(slot[:, :], rt[:, 3, :]).then_inc(route_ready, 1)
            own.step(dve, dve.tensor_scalar(ids_f[:, :], tile_no[:, :], ends[:, 0:1], None, ALU.is_ge))
            for e in range(1, E - 1):
                own.step(dve, dve.scalar_tensor_tensor(out=ids_f[:, :], in0=tile_no[:, :], scalar=ends[:, e:e + 1],
                                                       in1=ids_f[:, :], op0=ALU.is_ge, op1=ALU.add))
            dve.tensor_copy(ids[:, :], ids_f[:, :]).then_inc(route_ready, 1)
            dve.wait_ge(emx_ready, 1)
            own.step(dve, dve.tensor_scalar(rt[:, 4, :], emx, 1.0, None, ALU.add))
            own.step(dve, dve.reciprocal(alpha[:, :], rt[:, 4, :]))

            def view(t):
                return t.rearrange("p (g r h) -> p g r h", g=H, h=H)

            def keys(t):
                return t.rearrange("p r g -> p g r").unsqueeze(3).broadcast_to([P, H, HP, H])

            def queries(t):
                return t.unsqueeze(1).broadcast_to([P, H, HP, H])

            def scores_of(n, q):
                m, p0 = (q // 2) % 2, HP * (q % 2)
                if q % 2 == 0:
                    dve.wait_ge(ready["qkvw"], n * 2 + 4)
                if not (isinstance(n, int) and n == 0):
                    dve.wait_ge(exp_ready, n)
                if not (isinstance(n, int) and n < 3):
                    dve.wait_ge(f_ready, n - 2)
                for d, dst in ((0, A), (1, Bb)):
                    ins = dve.tensor_tensor(view(dst[:, :]), queries(QK[:, m, d, 0, p0:p0 + HP, :]),
                                            keys(QK[:, m, d, 1, p0:p0 + HP, :]), ALU.mult)
                own.step(dve, ins)
                own.step(dve, dve.tensor_tensor(A[:, :], A[:, :], Bb[:, :], ALU.add))
                own.step(dve, dve.tensor_reduce(Bb[:, 0:N], A[:, :].rearrange("p (g n) -> p n g", g=H), AX_X, ALU.max))
                dve.tensor_tensor(A[:, :].rearrange("p (g n) -> p g n", g=H), A[:, :].rearrange("p (g n) -> p g n", g=H),
                                  Bb[:, 0:N].unsqueeze(1).broadcast_to([P, H, N]), ALU.subtract).then_inc(s_ready, 1)

            def exp_v(n, q, folded=0):
                m, p0 = q // 2, HP * (q % 2)
                if q % 2 == 0:
                    dve.wait_ge(vw_ready, n * 2 + 4)
                dve.wait_ge(exp_ready, n + 1)
                if not (isinstance(n, int) and n < 2):
                    dve.wait_ge(sum_ready, n - 1)
                for d in range(2):
                    ins = dve.tensor_tensor(view(EXY[:, q % 2, 1 + d, :]), view(EXY[:, q % 2, 0, :]),
                                            keys(VW[:, m, d, 0, p0:p0 + HP, :]), ALU.mult)
                if folded:
                    own.step(dve, ins)
                    lo, hi = EXY[:, q % 2, 3 - folded:, 0:SZ // 2], EXY[:, q % 2, 3 - folded:, SZ // 2:]
                    ins = dve.tensor_tensor(lo, lo, hi, ALU.add)
                ins.then_inc(ev_ready, 1)

            def finish(bg, q):
                n = bg * NQ + q
                i, p0 = q // 2, HP * (q % 2)
                dve.wait_ge(sum_ready, n + 1)
                bank_ = sums[q % 2]
                own.step(dve, dve.reciprocal(rden[:, :], bank_[:, 0:N]))
                if isinstance(n, int) and n + 3 > NBG * NQ:
                    dve.wait_ge(s_ready, NBG * NQ)
                else:
                    dve.wait_ge(s_ready, n + 3)
                own.step(dve, dve.tensor_tensor(osb[:, :, :], bank_[:, N:3 * N].rearrange("p (d n) -> p d n", d=2),
                                                rden[:, :].unsqueeze(1).broadcast_to([P, 2, N]), ALU.mult))
                if q == 0 and not isinstance(bg, int) or q == 0 and bg:
                    dve.wait_ge(filled["oT"], bg * 4)
                dst = O[:, :, i * C + 2 * p0:i * C + 2 * p0 + 2 * HP].rearrange("p h (r d) -> p d r h", d=2)
                dve.tensor_tensor(dst, osb[:, :, :].rearrange("p d (r h) -> p d r h", h=H),
                                  VW[:, i, :, 1, p0:p0 + HP, :], ALU.mult).then_inc(f_ready, 1)

            dve.wait_ge(zeroed, 16 * ZERO_DMAS)
            scores_of(0, 0)
            scores_of(1, 1)
            dve.wait_ge(b1_ps, 1)
            w1v = W1s.rearrange("p (e c) -> p e c", e=E)
            dve.tensor_tensor(w1v[:, :, F:], out_ps[:, 0:E * FC].rearrange("p (e c) -> p e c", e=E),
                      b1T.rearrange("p (e c) -> p e c", e=E), ALU.add).then_inc(w1_ready, 1)
            exp_v(0, 0)

            def gate_in(bg, i):
                dve.wait_ge(fxn_ready, bg * NI + i + 1)
                for k in range(4):
                    t = bg * 4 + i * BGT + k
                    ins = dve.scalar_tensor_tensor(
                        out=fin_z[i][:, k * D:(k + 1) * D], in0=f_all[:, bass.ds(t * D, D)],
                        scalar=alpha[:, bass.ds(t, 1)], in1=fin_n[i][:, k * D:(k + 1) * D],
                        op0=ALU.mult, op1=ALU.add)
                ins.then_inc(z_ready, 1)

            def body(bg, turn):
                last, fold = turn is None and bg == NBG - 1, folds(bg, turn)
                for q in range(NQ):
                    if last and q == NQ - 1:
                        dve.wait_ge(exp_ready, NBG * NQ)
                        dve.wait_ge(gathered[0], 16 * BGT)
                        gate_in(0, 0)
                    if not last or q < NQ - 2:
                        scores_of(bg * NQ + q + 2, (q + 2) % NQ)
                    if not last or q < NQ - 1:
                        exp_v(bg * NQ + q + 1, (q + 1) % NQ, fold[q])
                    finish(bg, q)

            body(0, None)
            with dve.Fori(0, len(LOOP_BGS)) as turn:
                own.turn(turn, NQ * 6)
                body(turn + LOOP_BGS[0], turn)
            own.left(len(LOOP_BGS))
            body(NBG - 1, None)

            def gated(bg, i):
                w = bg * NI + i
                s = last_ps[i][:, :] if isinstance(bg, int) else s_all[:, bass.ds(w * NF, NF)]
                dve.wait_ge(sg_ready, w + 1)
                own.step(dve, dve.tensor_tensor(fin_z[i], fin_z[i], s, ALU.mult))
                dve.wait_ge(res_out[i], (bg + 1) * 16)
                dve.tensor_tensor(fin_r[i], fin_z[i], fin_x[i], ALU.add).then_inc(res_ready, 1)

            dve.wait_ge(gathered[1], 16 * (NT - BGT))
            dve.wait_ge(proj_ready, (NBG - 1) * NI + 1)
            with dve.Fori(0, NBG - 1) as bg:
                own.turn(bg, NI)
                for i in range(NI):
                    gate_in(bg + (i + 1) // NI, (i + 1) % NI)
                    gated(bg, i)
            own.left(NBG - 1)
            for i in range(NI):
                if i + 1 < NI:
                    gate_in(NBG - 1, i + 1)
                dve.wait_ge(proj_ps, (NBG - 1) * NI + i + 1)
                gated(NBG - 1, i)


INS = ['L0_attn_x', 'L0_attn_w_qkvw', 'L0_attn_w_out', 'L0_ffn_centroids', 'L0_ffn_gamma', 'L0_ffn_beta',
       'L0_ffn_W1', 'L0_ffn_b1', 'L0_ffn_W2', 'L0_ffn_b2']


def kernel(**inputs):
    import numpy as np
    import concourse.bacc as bacc
    from concourse.bass_utils import run_bass_kernel_spmd

    nc = bacc.Bacc("TRN2", target_bir_lowering=False, num_devices=1)
    arrays, args = {}, []
    for name in INS:
        a = np.ascontiguousarray(inputs[name])
        arrays[f"in_{name}"] = a
        args.append(nc.dram_tensor(f"in_{name}", a.shape, mybir.dt.from_np(a.dtype), kind="ExternalInput").ap())
    out = nc.dram_tensor("out", inputs["L0_attn_x"].shape, F32, kind="ExternalOutput").ap()
    program(nc, *args, out)
    r = run_bass_kernel_spmd(nc, [arrays], core_ids=[0])
    return r.results[0]["out"]
```

```python
from contextlib import ExitStack

import concourse.bass as bass
from concourse import mybir

F32 = mybir.dt.float32
BF16 = mybir.dt.bfloat16
I32 = mybir.dt.int32
U32 = mybir.dt.uint32
ALU = mybir.AluOpType
ACT = mybir.ActivationFunctionType
AX_X = mybir.AxisListType.X

P = 128
D = 128
B, S = 32, 256
NT = B * S // P
H = 16
NI = 4
NR = 4
C = D // NI
NP = C // 2
SCALE = 2.0 ** -0.5
EPS = 1e-5

E = 8
F = 512
FC = F // P
FT = 72
FTL = FT + 4
NW1 = 3
W1C = F + FC

GT = 8
NG = NT // GT

NBG = 4
BGT = NT // NBG
HP = NP // 2
N = HP * H
SZ = H * N
NQ = 2 * NI
LOOP_BGS = (1, 2)
FFN_FIRST = [0] * 4 + [3] * 4
FFN_LOOP = [4, 4, 4, 3] * 2
PER_BG = sum(FFN_LOOP)
assert sum(FFN_FIRST) + PER_BG * len(LOOP_BGS) == FT
FOLD_FIRST, FOLD_LOOP, FOLD_LAST = [0] * 4 + [1] * 4, [2, 1] * 4, [0] * (NQ - 3) + [2, 3, 3]
PROJECT_AT = ((1, 2), (1, 3), (2, 0), (2, 1))
START_EXPERTS = (3, 1)
EXP_BEHIND, SUM_BEHIND = 1, 3
ZERO_DMAS = -(-FTL * D // SZ)


class Count:

    def __init__(self, sem):
        self.sem, self.n, self.base = sem, 0, 0

    def inc(self, ins):
        ins.then_inc(self.sem, 1)
        self.n += 1

    def wait(self, eng):
        eng.wait_ge(self.sem, self.base + self.n)

    def step(self, eng, ins):
        self.inc(ins)
        self.wait(eng)

    def turn(self, it, per):
        self.start, self.per, self.base = self.n, per, it * per

    def left(self, turns):
        assert self.n - self.start == self.per, (self.n - self.start, self.per)
        self.n, self.base = self.start + turns * self.per, 0


def work_uses(bg, last):
    uses = []
    for q in range(NQ):
        m = q // 2
        if q == 4 and not last:
            uses += [(q, "xT", bg + 1, j) for j in range(4)]
        if q % 2 == 1 and (m < 2 or not last):
            uses += [(q, "qkvw", bg * NI + m + 2, j) for j in range(4)]
    return uses + [(NQ, "oT", bg, j) for j in range(4)]


def program(nc, x, w_qkvw, w_out, centroids, gamma, beta, W1, b1, W2, b2, out):
    with ExitStack() as ctx:
        def sb(name, shape, dt=F32):
            return ctx.enter_context(nc.sbuf_tensor(name, shape, dt))

        def sem(name):
            return ctx.enter_context(nc.semaphore(name))

        xs_dram = nc.dram_tensor("xs_dram", [FTL * P, D], F32, kind="Internal").ap()
        y_dram = nc.dram_tensor("y_dram", [FT * P, D], F32, kind="Internal").ap()

        xf = x.rearrange("b s d -> (b s) d")
        outf = out.rearrange("b s d -> (b s) d")

        A = sb("A", [P, SZ])
        Bb = sb("Bb", [P, SZ])
        EXY = sb("EXY", [P, 2, 3, SZ])
        QK = sb("QK", [P, 2, 2, 2, NP, H])
        VW = sb("VW", [P, NI, 2, 2, NP, H])
        x_bg = sb("x_bg", [P, BGT, D])
        xnT = sb("xnT", [P, BGT * P])
        OO = sb("OO", [P, 2 * H * D])
        OJ = x_bg[:, :, :].rearrange("p (i k) d -> p i (k d)", i=NI)
        O = OO[:, 0:H * D].rearrange("p (h c) -> p h c", h=H)
        OT = OO[:, H * D:]
        xhat = sb("xhat", [P, NT * D])
        s_all = xhat
        WW = sb("WW", [P, E * W1C + E * F])
        W1s = WW[:, 0:E * W1C]
        W2s = WW[:, E * W1C:]
        f_all = WW[:, 0:NT * D]
        w1slot = sb("w1slot", [P, NW1, W1C])
        xs = sb("xs", [P, 2, D])
        xsT = sb("xsT", [P, 2, P])
        hT = sb("hT", [P, 2, FC, P])
        ysb = sb("ysb", [P, 2, D])
        wq = sb("wq", [P, NI * NR * C])
        wo = sb("wo", [P, D])
        ident = sb("ident", [P, P])
        perm = sb("perm", [P, P])
        row0 = sb("row0", [P, P])
        eps = sb("eps", [P, 1])
        b2row = sb("b2row", [P, E * D])
        RS = sb("RS", [P, NT])
        NM = sb("NM", [P, NT])
        alpha = sb("alpha", [P, NT])
        slot = sb("slot", [P, NT], U32)
        ids = sb("ids", [P, FTL], I32)
        rden = sb("rden", [P, N])
        idle = sb("idle", [P, 1])
        osb = Bb[:, SZ - 2 * N:].rearrange("p (d n) -> p d n", d=2)
        tot_i = sb("tot_i", [P, E], I32)

        flat = EXY[:, :, :, :].rearrange("p a b n -> p (a b n)")
        G = GT * D
        x_st = flat[:, 0:NT * D]
        xn_st = [v.rearrange("p (k d) -> p k d", k=GT) for v in (A[:, 0:G], A[:, G:2 * G], flat[:, NT * D:NT * D + G])]
        xnT_g = QK[:, :, :, :, :, :].rearrange("p a b c r h -> p (a b c r h)")[:, 0:GT * P]
        zeros = Bb
        taken = 0

        def early(cols):
            nonlocal taken
            taken += cols
            assert taken <= 2 * H * D
            return OO[:, taken - cols:taken]

        scores = early(NT * E).rearrange("p (t e) -> p t e", e=E)
        eq = early(NT * E).rearrange("p (t e) -> p t e", e=E)
        ohb = early(NT * E // 2).bitcast(BF16).rearrange("p (t e) -> p t e", e=E)
        ahead = early((NT + 1) * E // 2).bitcast(BF16)[0:NT, :]
        mx, best, emx, slot_f, den = (early(NT) for _ in range(5))
        rank = early(E)
        tiles, ends_a, ends_b, base = (early(E) for _ in range(4))
        tile_no, ids_f = early(FTL), early(FTL)
        tri = early(P // 2).bitcast(BF16)
        onesb = early(P // 2).bitcast(BF16)
        small = early(D)[0:3 * E + E * FC, :]
        smallT = early(3 * E + E * FC)
        cT, gT, bT = (smallT[:, E * n:E * n + E] for n in range(3))
        b1T = smallT[:, 3 * E:]
        st = early(6 * GT).rearrange("p (k n) -> p k n", n=6)
        mv = early(6 * GT).rearrange("p (s k n) -> p s k n", s=3, n=2)
        dev, rs, nm, sq, dev2, rs2 = (early(3 * GT).rearrange("p (s k) -> p s k", s=3) for _ in range(6))

        bank = [ctx.enter_context(nc.psum_tensor(f"bank{n}", [P, 512], F32)) for n in range(8)]
        work = bank[0:2]
        sums = bank[2:4]
        hT_ps, xsT_ps, y_ps, out_ps = last_ps = bank[4:8]

        def sems(*names):
            return [sem(n) for n in names]

        small_in, w_in, wraw_in, xbg_in = sems("small_in", "w_in", "wraw_in", "xbg_in")
        x_in = sems("x_in0", "x_in1", "x_in2")
        zeroed, scattered = sems("zeroed", "scattered")
        gathered = sems("gathered_first", "gathered_rest")
        consts, dve_own, pool_own = sems("consts", "dve_own", "pool_own")
        smallT_ps, smallT_ready = sems("smallT_ps", "smallT_ready")
        var1, dev1, var2, dev_2, rs2_ready = sems("var1_ready", "dev1_ready", "var2_ready", "dev2_ready", "rs2_ready")
        xn_ready, xnT_ps, xnT_sb, xhat_ready = sems("xn_ready", "xnT_ps", "xnT_sb", "xhat_ready")
        sc_ps, sc_ready = sems("sc_ps", "sc_ready")
        mx_ready, emx_ready, oh_ready, prefix_ps, ahead_ready = sems("mx_ready", "emx_ready", "oh_ready", "prefix_ps",
                                                                     "ahead_ready")
        route_ready = sem("route_ready")
        wT_ps, wT_ready, b1_ps, w1_ready = sems("wT_ps", "wT_ready", "b1_ps", "w1_ready")
        xnb_ready = sem("xnb_ready")
        filled = {k: sem(k + "_ps") for k in ("qkvw", "xT", "oT")}
        ready = {k: sem(k + "_ready") for k in ("qkvw", "xT", "oT")}
        vw_ready = sem("vw_ready")
        s_ready, exp_ready, ev_ready, sum_ready, f_ready = sems("s_ready", "exp_ready", "ev_ready", "sum_ready", "f_ready")
        oj_in, proj_ps, proj_ready = sems("oj_in", "proj_ps", "proj_ready")
        xs_in, y_out = sems("xs_in0", "xs_in1"), sems("y_out0", "y_out1")
        w1_in = [sem(f"w1_in{n}") for n in range(NW1)]
        xsT_full, xsT_ready, h_full, h_ready, y_full, y_ready = sems("xsT_full", "xsT_ready", "h_full", "h_ready",
                                                                     "y_full", "y_ready")
        fx_in, res_out = ([sem(f"{k}{i}") for i in range(NI)] for k in ("fx_in", "res_out"))
        fxn_ready, z_ready, sg_ready, res_ready = sems("fxn_ready", "z_ready", "sg_ready", "res_ready")

        block = ctx.enter_context(nc.Block())

        def bgs(eng, body):
            body(0, None)
            with eng.Fori(0, len(LOOP_BGS)) as turn:
                body(turn + LOOP_BGS[0], turn)
            body(NBG - 1, None)

        def groups(eng, step):
            step(0, 0, 0)
            with eng.Fori(0, (NG - 2) // 3) as it:
                for j in range(1, 4):
                    step(it * 3 + j, j % 3, it + j // 3)
            step(NG - 1, (NG - 1) % 3, (NG - 1) // 3)

        def ffn_tiles(bg, turn):
            if turn is None and bg == NBG - 1:
                return [[]] * NQ
            k, at = (0, 0) if turn is None else (sum(FFN_FIRST), turn * PER_BG)
            steps = []
            for n in FFN_FIRST if turn is None else FFN_LOOP:
                steps.append([(at + k + j, k + j, 0 if turn is None else turn) for j in range(n)])
                k += n
            return steps

        def folds(bg, turn):
            return FOLD_LOOP if turn is not None else FOLD_FIRST if bg == 0 else FOLD_LAST

        def nth_use(j, turn, slots):
            return turn * (PER_BG // slots) + j // slots + 1

        NF = 4 * D
        qk_flat = QK[:, :, :, :, :, :].rearrange("p a b c r h -> p (a b c r h)")
        fin_x, fin_z, fin_n, fin_r = ([buf[:, i * NF:(i + 1) * NF] for i in range(NI)] for buf in (xnT, A, Bb, qk_flat))

        def fin_rows(ap, bg, i):
            t0 = i * BGT + bg * 4
            return ap[bass.ds(t0 * P, NF // D * P), :].rearrange("(k p) d -> p k d", p=P)

        @block.sync
        def _(sp):
            for g in range(NG):
                if g >= 3:
                    sp.wait_ge(x_in[g % 3], g // 3 * 16)
                sp.dma_start(x_st[:, g * G:(g + 1) * G].rearrange("p (k d) -> p k d", k=GT),
                             xf[g * GT * P:(g + 1) * GT * P, :].rearrange("(k p) d -> p k d", p=P))\
                    .then_inc(x_in[g % 3], 16)
            sp.dma_start(wq[:, :], w_qkvw).then_inc(w_in, 16)
            sp.dma_start(wo[:, :], w_out).then_inc(w_in, 16)
            sp.wait_ge(consts, 8)
            sp.dma_start(b2row[0:1, :], b2.rearrange("(a e) d -> a (e d)", a=1)).then_inc(w_in, 16)

            def load_bg(bg):
                for k in range(0, BGT, GT):
                    sp.dma_start(x_bg[:, k:k + GT, :], xf[bass.ds(bg * (BGT * P) + k * P, GT * P), :]
                                 .rearrange("(k p) d -> p k d", p=P)).then_inc(xbg_in, 16)

            load_bg(0)
            for e in range(E):
                sp.dma_start(W1s[:, e * W1C:e * W1C + F].rearrange("p (c d) -> p c d", d=D),
                             W1[e, :, :].rearrange("(c p) d -> p c d", p=P)).then_inc(wraw_in, 16)
            sp.dma_start(W2s.rearrange("p (e f) -> p e f", f=F), W2.rearrange("e n f -> n e f")).then_inc(wraw_in, 16)

            def load_xs(k, j):
                sp.dma_start(xs[:, j % 2, :], xs_dram[bass.ds(k * P, P), :]).then_inc(xs_in[j % 2], 16)

            def load_w1(k, j):
                e = sp.value_load(ids[0:1, bass.ds(k, 1)], min_val=0, max_val=E - 1)
                sp.dma_start(w1slot[:, j % NW1, :], W1s[:, bass.ds(e * W1C, W1C)]).then_inc(w1_in[j % NW1], 16)

            for s in range(2):
                sp.sem_inc(y_out[s], 16)
            for i in range(NI):
                sp.sem_inc(res_out[i], 16)

            def body(bg, turn):
                if turn is None and bg == NBG - 1:
                    return
                if turn is None:
                    sp.wait_ge(filled["xT"], 4)
                    load_bg(1)
                    sp.wait_ge(route_ready, 2)
                    sp.wait_ge(w1_ready, 2)
                    sp.wait_ge(scattered, 16 * NT)
                    for k in range(2):
                        load_xs(k, k)
                        load_w1(k, k)
                    load_w1(2, 2)
                    for k in range(2, 4):
                        sp.wait_ge(xsT_full, k - 1)
                        load_xs(k, k)
                    sp.wait_ge(h_ready, FC)
                    load_w1(3, 3)
                for q, steps in enumerate(ffn_tiles(bg, turn)):
                    if q == 3 and turn is not None:
                        sp.wait_ge(proj_ps, bg * NI)
                        load_bg(bg + 1)
                    for k, j, _ in steps:
                        sp.wait_ge(xsT_full, k + 3)
                        load_xs(k + 4, j + 4)
                        sp.wait_ge(h_ready, (k + 2) * FC)
                        load_w1(k + 4, j + 4)
                        sp.wait_ge(y_ready, k + 2)
                        sp.dma_start(y_dram[bass.ds(k * P, P), :], ysb[:, j % 2, :]).then_inc(y_out[j % 2], 16)

            bgs(sp, body)

            def load_fin(bg, i):
                sp.dma_start(fin_x[i].rearrange("p (k d) -> p k d", d=D), fin_rows(xf, bg, i)).then_inc(fx_in[i], 16)

            def store_fin(bg, i):
                sp.wait_ge(res_ready, bg * NI + i + 1)
                sp.dma_start(fin_rows(outf, bg, i), fin_r[i].rearrange("p (k d) -> p k d", d=D))\
                    .then_inc(res_out[i], 16)

            sp.wait_ge(filled["qkvw"], NBG * NI * 4)
            for i in range(NI):
                load_fin(0, i)
            with sp.Fori(0, NBG - 1) as bg:
                for i in range(NI):
                    store_fin(bg, i)
                    load_fin(bg + 1, i)
            for i in range(NI):
                store_fin(NBG - 1, i)
            for i in range(NI):
                sp.wait_ge(res_out[i], 16 * (1 + NBG))

        @block.gpsimd
        def _(pool):
            own = Count(pool_own)
            own.inc(pool.memset(ident[:, :], 0.0))
            own.inc(pool.memset(tri[:, :], 1.0))
            pool.memset(onesb[:, :], 1.0).then_inc(consts, 1)
            own.inc(pool.memset(row0[:, :], 0.0))
            own.inc(pool.memset(b2row[:, :], 0.0))
            pool.memset(eps[:, :], EPS).then_inc(consts, 1)
            own.wait(pool)
            pool.affine_select(out=ident[:, :], in_=ident[:, :], compare_op=ALU.not_equal, fill=1.0, base=0,
                               pattern=[[-1, P]], channel_multiplier=1).then_inc(consts, 1)
            pool.memset(row0[0:1, :], 1.0).then_inc(consts, 1)
            pool.wait_ge(consts, 4)
            pool.tensor_copy(perm[:, :].rearrange("p (j m) -> p j m", j=4),
                             ident[:, :].rearrange("p (m j) -> p j m", j=4)).then_inc(consts, 1)
            pool.affine_select(out=tri[:, :], in_=tri[:, :], compare_op=ALU.is_gt, fill=0.0, base=0,
                               pattern=[[1, P]], channel_multiplier=-1).then_inc(consts, 1)
            pool.iota(rank, [[-1, E]], base=E, channel_multiplier=0,
                      allow_small_or_imprecise_dtypes=True).then_inc(consts, 1)
            pool.iota(tile_no[:, :], [[1, FTL]], base=0, channel_multiplier=0,
                      allow_small_or_imprecise_dtypes=True).then_inc(consts, 1)
            own.step(pool, pool.memset(zeros[:, :], 0.0))
            pool.wait_ge(xn_ready, 4)
            flat_xs = xs_dram.rearrange("(p r) d -> p (r d)", p=P)
            per, at = FTL * D, 0
            while at < per:
                n = min(SZ, per - at)
                pool.dma_start(flat_xs[:, at:at + n], zeros[:, 0:n]).then_inc(zeroed, 16)
                at += n
            pool.wait_ge(zeroed, 16 * ZERO_DMAS)

            def scatter(t):
                pool.indirect_dma_start(out=xs_dram, out_offset=bass.IndirectOffsetOnAxis(ap=slot[:, t:t + 1], axis=0),
                                        in_=xhat[:, t * D:(t + 1) * D], in_offset=None).then_inc(scattered, 16)

            pool.wait_ge(route_ready, 1)
            pool.wait_ge(xhat_ready, NG)
            for t in range(NT):
                scatter(t)

            def swap(bg):
                pool.wait_ge(ready["oT"], bg * 4 + 4)
                if bg < NBG - 1:
                    pool.wait_ge(filled["xT"], (bg + 2) * 4)
                if bg:
                    pool.wait_ge(proj_ps, bg * NI)
                for i in range(NI):
                    for j in range(4):
                        pool.dma_start(OJ[C * j:C * j + C, i, :], OT[C * i:C * i + C, 4 * P * j:4 * P * (j + 1)])\
                            .then_inc(oj_in, 16)

            for bg in range(NBG - 1):
                swap(bg)

            for s in range(2):
                pool.wait_ge(y_out[s], 16 * (1 + FT // 2))
            pool.wait_ge(h_full, FT + 1)
            for s in range(NW1):
                pool.wait_ge(w1_in[s], 16 * (FT // NW1 + (4 + NW1 - 1 - s) // NW1))
            order = [i * BGT + b * 4 + k for b in range(NBG) for i in range(NI) for k in range(4)]
            for m, t in enumerate(order):
                pool.indirect_dma_start(out=f_all[:, t * D:(t + 1) * D], out_offset=None, in_=y_dram,
                                        in_offset=bass.IndirectOffsetOnAxis(ap=slot[:, t:t + 1], axis=0))\
                    .then_inc(gathered[m >= BGT], 16)
            swap(NBG - 1)

        @block.scalar
        def _(act):
            for n, w in enumerate((centroids, gamma, beta)):
                act.dma_start(small[E * n:E * n + E, :], w).then_inc(small_in, 16)
            act.dma_start(small[3 * E:, :], b1.rearrange("e (c f) -> (e c) f", c=FC)).then_inc(small_in, 16)
            act.wait_ge(smallT_ps, 1)
            act.activation(smallT[:, :], work[0][:, 0:3 * E + E * FC], ACT.Copy).then_inc(smallT_ready, 1)

            act.wait_ge(consts, 8)

            def deviation(g, s):
                act.wait_ge(var1, g + 1)
                act.activation(dev[:, s, :], mv[:, s, :, 1], ACT.Sqrt, bias=eps[:, 0:1]).then_inc(dev1, 1)

            def copy_scores(g):
                act.wait_ge(sc_ps, g + 1)
                act.activation(scores[:, bass.ds(g * GT, GT), :].rearrange("p t e -> p (t e)"), out_ps[:, 0:GT * E],
                               ACT.Copy).then_inc(sc_ready, 1)

            def second_norm(g, s):
                act.wait_ge(rs2_ready, g + 1)
                for k in range(GT):
                    ins = act.activation(xhat[:, bass.ds(g * (GT * D) + k * D, D)], xn_st[s][:, k, :], ACT.Copy,
                                         scale=rs2[:, s, k:k + 1])
                ins.then_inc(xhat_ready, 1)

            def group(g, s, first=False):
                act.wait_ge(var2, g + 1)
                act.activation(dev2[:, s, :], sq[:, s, :], ACT.Sqrt, bias=eps[:, 0:1]).then_inc(dev_2, 1)
                if not first:
                    second_norm(g - 1, (s - 1) % 3)
                    copy_scores(g - 1)
                for j in range(2):
                    act.wait_ge(xnT_ps, g * 2 + j + 1)
                    if j == 0 and not first:
                        act.wait_ge(sc_ps, g)
                    act.activation(xnT_g[:, 512 * j:512 * j + 512], work[j][:, :], ACT.Copy).then_inc(xnT_sb, 1)
            deviation(0, 0)
            deviation(1, 1)
            group(0, 0, True)
            with act.Fori(0, (NG - 2) // 3) as it:
                for j in range(1, 4):
                    g = it * 3 + j
                    deviation(g + 1, (j + 1) % 3)
                    group(g, j % 3)
            group(NG - 1, (NG - 1) % 3)
            second_norm(NG - 1, (NG - 1) % 3)
            copy_scores(NG - 1)
            def evac_w(u):
                act.wait_ge(wT_ps, u + 1)
                e = u % E
                dst = W1s[:, e * W1C:e * W1C + F] if u < E else W2s[:, e * F:(e + 1) * F]
                act.activation(dst, work[u % 2][:, :], ACT.Copy).then_inc(wT_ready, 1)

            def fin_norm(bg, i):
                act.wait_ge(fx_in[i], (bg + 1) * 16)
                for k in range(4):
                    t = bg * 4 + i * BGT + k
                    ins = act.activation(fin_n[i][:, k * D:(k + 1) * D], fin_x[i][:, k * D:(k + 1) * D],
                                         ACT.Identity, scale=RS[:, bass.ds(t, 1)], bias=NM[:, bass.ds(t, 1)])
                ins.then_inc(fxn_ready, 1)

            def gate(bg, i):
                act.wait_ge(z_ready, bg * NI + i + 1)
                act.activation(fin_z[i], fin_z[i], ACT.Silu).then_inc(sg_ready, 1)

            def normalise(bg):
                act.wait_ge(xbg_in, (bg + 1) * (16 * BGT // GT))
                for k in range(BGT):
                    t = bg * BGT + k
                    ins = act.activation(x_bg[:, k, :], x_bg[:, k, :], ACT.Identity, scale=RS[:, bass.ds(t, 1)],
                                         bias=NM[:, bass.ds(t, 1)])
                ins.then_inc(xnb_ready, 1)

            def evac(kind, n, j, u, i=0):
                act.wait_ge(filled[kind], n * 4 + j + 1)
                src = work[u % 2]
                if kind == "xT":
                    if not isinstance(n, int) or n:
                        act.wait_ge(filled["qkvw"], n * 4 * NI)
                    tok = xnT[:, :].rearrange("p (h b a) -> p b h a", h=H, a=H)
                    dst = tok[:, 2 * j:2 * j + 2, :, :]
                    src = src[:, :].rearrange("p (b h a) -> p b h a", b=2, h=H)
                elif kind == "oT":
                    if not isinstance(n, int) or n:
                        act.wait_ge(oj_in, n * (16 * NI * 4))
                    dst = OT.rearrange("p (m h a) -> p h m a", h=H, a=4)[:, 4 * j:4 * j + 4, :, :]
                    src = src[:, :].rearrange("p (h m a) -> p h m a", h=4, a=4)
                else:
                    if not isinstance(n, int) or n >= 2:
                        act.wait_ge(s_ready, n * 2 - 2)
                    if not isinstance(n, int) or n >= NI:
                        act.wait_ge(f_ready, n * 2 - 6)
                    hh = H // 4
                    src = src[:, :].rearrange("p (h rc d) -> p d rc h", h=hh, d=2)
                    dst = VW[:, i, :, :, :, hh * j:hh * j + hh].rearrange("p d r c h -> p d (r c) h")
                    act.activation(dst, src[:, :, 2 * NP:, :], ACT.Copy).then_inc(vw_ready, 1)
                    dst = QK[:, i % 2, :, :, :, hh * j:hh * j + hh].rearrange("p d r c h -> p d (r c) h")
                    src = src[:, :, 0:2 * NP, :]
                act.activation(dst, src, ACT.Copy).then_inc(ready[kind], 1)

            def exp(n, q):
                act.wait_ge(s_ready, n + 1)
                if not (isinstance(n, int) and n < 2):
                    act.wait_ge(sum_ready, n - 1)
                act.activation(EXY[:, q % 2, 0, :], A[:, :], ACT.Exp, scale=SCALE).then_inc(exp_ready, 1)

            def evac_xsT(k, j):
                act.wait_ge(xsT_full, k + 1)
                if not (isinstance(k, int) and k < 2):
                    act.wait_ge(h_full, k - 1)
                act.activation(xsT[:, j % 2, :], xsT_ps[:, 0:P], ACT.Copy).then_inc(xsT_ready, 1)

            def relu(k, j):
                act.wait_ge(h_full, k + 1)
                if not (isinstance(k, int) and k < 2):
                    act.wait_ge(y_full, k)
                for c in range(FC):
                    act.activation(hT[:, j % 2, c, :], hT_ps[:, c * P:(c + 1) * P], ACT.Relu,
                                   bias=w1slot[:, j % NW1, F + c:F + c + 1]).then_inc(h_ready, 1)

            def evac_y(k, j, turn):
                act.wait_ge(y_full, k + 2)
                act.wait_ge(y_out[j % 2], nth_use(j, turn, 2) * 16)
                act.activation(ysb[:, j % 2, :], y_ps[:, 0:D], ACT.Copy).then_inc(y_ready, 1)

            def ffn_tile(k, j, turn):
                evac_xsT(k + 2, j + 2)
                relu(k + 1, j + 1)
                evac_y(k, j, turn)

            act.sem_inc(y_ready, 1)
            act.sem_inc(proj_ready, 1)
            for j in range(4):
                evac("xT", 0, j, j)
            act.wait_ge(mx_ready, 1)
            act.activation(emx, mx, ACT.Exp, scale=-1.0).then_inc(emx_ready, 1)
            for c in range(2):
                for j in range(4):
                    evac("qkvw", c, j, j, c)
            for u in range(E):
                evac_w(u)
            exp(0, 0)
            act.wait_ge(b1_ps, 1)
            for e in range(E):
                ins = act.activation(W1s[:, e * W1C:e * W1C + F], W1s[:, e * W1C:e * W1C + F], ACT.Copy,
                                     scale=gT[:, e:e + 1])
            ins.then_inc(w1_ready, 1)
            exp(1, 1)
            for u in range(E, 2 * E):
                evac_w(u)

            def evac_proj(bg, i):
                w = bg * NI + i
                act.wait_ge(scattered, 16 * NT)
                act.wait_ge(proj_ps, w + 1)
                act.activation(s_all[:, bass.ds(w * 512, 512)], out_ps[:, :], ACT.Copy).then_inc(proj_ready, 1)

            def body(bg, turn):
                first, last = turn is None and bg == 0, turn is None and bg == NBG - 1
                uses = work_uses(bg, last)
                ffn = ffn_tiles(bg, turn)
                for q in range(NQ + 1):
                    if last and q == NQ:
                        act.wait_ge(s_ready, NBG * NQ)
                        fin_norm(0, 0)
                        fin_norm(0, 1)
                        gate(0, 0)
                    for u, (qq, kind, n, j) in enumerate(uses):
                        if qq == q:
                            evac(kind, n, j, u, (q // 2 + 2) % NI)
                    if q == NQ:
                        break
                    for m in range(max(FFN_LOOP)):
                        if m < len(ffn[q]):
                            ffn_tile(*ffn[q][m])
                        if m == EXP_BEHIND and (not last or q < NQ - 2):
                            exp(bg * NQ + q + 2, q)
                        if first and (q, m) == START_EXPERTS:
                            evac_xsT(0, 0)
                            evac_xsT(1, 1)
                            relu(0, 0)
                        if (q, m) in PROJECT_AT and not first:
                            evac_proj(bg - 1, PROJECT_AT.index((q, m)))
                    if q == (1 if first else 3) and not last:
                        normalise(bg + 1)

            bgs(act, body)

            act.wait_ge(f_ready, NBG * NQ)

            with act.Fori(0, NBG - 1) as bg:
                for i in range(NI):
                    fin_norm(bg + (i + 2) // NI, (i + 2) % NI)
                    gate(bg + (i + 1) // NI, (i + 1) % NI)
            for i in range(NI - 1):
                if i < 2:
                    fin_norm(NBG - 1, i + 2)
                gate(NBG - 1, i + 1)

        @block.tensor
        def _(pe):
            pe.wait_ge(consts, 8)
            pe.wait_ge(small_in, 64)
            rows = 3 * E + E * FC
            pe.transpose(work[0][:, 0:rows], small[:, :], ident[0:rows, 0:rows]).then_inc(smallT_ps, 1)
            pe.wait_ge(smallT_ready, 1)

            def group(g, s, m):
                first = isinstance(g, int) and g == 0
                pe.wait_ge(xn_ready, g + 1)
                for j in range(2):
                    if not first:
                        pe.wait_ge(xnT_sb, g * 2 + j - 1)
                    for k in range(4):
                        ins = pe.transpose(work[j][:, k * P:(k + 1) * P], xn_st[s][:, 4 * j + k, :], ident[:, :])
                    ins.then_inc(xnT_ps, 1)
                if not first:
                    pe.wait_ge(sc_ready, g)
                for k in range(GT):
                    if k % 4 == 0:
                        pe.wait_ge(xnT_sb, g * 2 + k // 4 + 1)
                    ins = pe.matmul(out_ps[:, k * E:(k + 1) * E], xnT_g[:, k * P:(k + 1) * P], cT,
                                    start=True, stop=True)
                ins.then_inc(sc_ps, 1)

            groups(pe, group)
            def transpose_w(u):
                e = u % E
                if u >= 2:
                    pe.wait_ge(wT_ready, u - 1)
                for c in range(FC):
                    src = W1s[:, e * W1C + c * P:e * W1C + (c + 1) * P] if u < E else \
                        W2s[:, e * F + c * P:e * F + (c + 1) * P]
                    ins = pe.transpose(work[u % 2][:, c * P:(c + 1) * P], src, ident[:, :])
                ins.then_inc(wT_ps, 1)

            def fill(kind, n, j, u, i=0):
                dst = work[u % 2]
                if kind == "xT":
                    if j == 0:
                        pe.wait_ge(xnb_ready, n + 1)
                    for k in range(4):
                        ins = pe.transpose(dst[:, k * P:(k + 1) * P], x_bg[:, 4 * j + k, :], ident[:, :])
                elif kind == "oT":
                    if j == 0:
                        pe.wait_ge(f_ready, n * NQ + NQ)
                    for k in range(4):
                        ins = pe.transpose(dst[:, k * P:(k + 1) * P], O[:, 4 * j + k, :], perm[:, :])
                else:
                    hh, tok = H // 4, xnT[:, :].rearrange("p (h n) -> p h n", h=H)
                    for h in range(hh):
                        ins = pe.matmul(dst[:, h * NR * C:(h + 1) * NR * C], tok[:, hh * j + h, :],
                                        wq[:, i * NR * C:(i + 1) * NR * C], start=True, stop=True)
                ins.then_inc(filled[kind], 1)

            def copied(kind, n, j):
                pe.wait_ge(ready[kind], n * 4 + j + 1)

            def sum_keys(n, q, folded=0):
                pe.wait_ge(ev_ready, n + 1)
                if not (isinstance(n, int) and n < 2):
                    pe.wait_ge(f_ready, n - 1)
                keys = H if folded < 3 else H // 2
                for g in range(keys):
                    parts = 3 - folded if g >= H // 2 else 3
                    ins = pe.matmul(sums[q % 2][:, 0:parts * N], ident[:, :], EXY[:, q % 2, 0:parts, g * N:(g + 1) * N],
                                    start=(g == 0), stop=(g == keys - 1))
                ins.then_inc(sum_ready, 1)

            def ffn_transpose(k, j, turn):
                pe.wait_ge(xs_in[j % 2], nth_use(j, turn, 2) * 16)
                if not (isinstance(k, int) and k < 1):
                    pe.wait_ge(xsT_ready, k)
                pe.transpose(xsT_ps[:, 0:P], xs[:, j % 2, :], ident[:, :]).then_inc(xsT_full, 1)

            def ffn_up(k, j, turn):
                pe.wait_ge(w1_in[j % NW1], nth_use(j, turn, NW1) * 16)
                pe.wait_ge(xsT_ready, k + 1)
                if not (isinstance(k, int) and k < 1):
                    pe.wait_ge(h_ready, k * FC)
                for c in range(FC):
                    ins = pe.matmul(hT_ps[:, c * P:(c + 1) * P], w1slot[:, j % NW1, c * P:(c + 1) * P],
                                    xsT[:, j % 2, :], start=True, stop=True)
                ins.then_inc(h_full, 1)

            def ffn_down(k, j):
                e = pe.value_load(ids[0:1, bass.ds(k, 1)], min_val=0, max_val=E - 1)
                pe.wait_ge(y_ready, k + 1)
                pe.matmul(y_ps[:, 0:D], row0[:, :], b2row[:, bass.ds(e * D, D)], start=True, stop=False)
                pe.wait_ge(h_ready, (k + 1) * FC)
                for c in range(FC):
                    ins = pe.matmul(y_ps[:, 0:D], hT[:, j % 2, c, :], W2s[:, bass.ds(e * F + c * P, D)],
                                    start=False, stop=(c == FC - 1))
                ins.then_inc(y_full, 1)

            def ffn_tile(k, j, turn):
                ffn_transpose(k + 2, j + 2, turn)
                ffn_up(k + 1, j + 1, turn)
                ffn_down(k, j)

            pe.sem_inc(y_full, 1)
            pe.wait_ge(w_in, 16 * 3)
            pe.wait_ge(xnT_sb, 2 * NG)
            for j in range(4):
                if j >= 2:
                    copied("xT", 0, j - 2)
                fill("xT", 0, j, j)
            copied("xT", 0, 3)
            pe.wait_ge(sc_ready, NG)
            pe.wait_ge(oh_ready, 1)
            for e in range(E):
                ins = pe.matmul(sums[1][0:NT, e:e + 1], ohb[:, :, e], onesb[:, 0:1], start=True, stop=True)
            ins.then_inc(prefix_ps, 1)
            pe.matmul(sums[0][:, :], tri[:, :], ohb, start=True, stop=False)
            pe.wait_ge(ahead_ready, 1)
            pe.matmul(sums[0][:, :], onesb[0:NT, :], ahead[:, 0:NT * E], start=False, stop=True)
            pe.matmul(out_ps[:, 0:E], onesb[0:NT, :], ahead[:, NT * E:], start=True, stop=True).then_inc(prefix_ps, 1)
            for c in range(2):
                for j in range(4):
                    if c or j >= 2:
                        copied("qkvw", (4 * c + j - 2) // 4, (j - 2) % 4)
                    fill("qkvw", c, j, j, c)
            pe.wait_ge(wraw_in, 16 * (E + 1))
            copied("qkvw", 1, 3)
            for u in range(E):
                transpose_w(u)
            pe.wait_ge(route_ready, 1)
            pe.wait_ge(wT_ready, E)
            for m in range(E * FC):
                e, c = m // FC, m % FC
                ins = pe.matmul(out_ps[:, m:m + 1], W1s[:, e * W1C + c * P:e * W1C + (c + 1) * P], bT[:, e:e + 1],
                                start=True, stop=True)
            ins.then_inc(b1_ps, 1)
            for u in range(E, 2 * E):
                transpose_w(u)
            sum_keys(0, 0)
            pe.wait_ge(wT_ready, 2 * E)

            def project(bg, i):
                w = bg * NI + i
                pe.wait_ge(w1_ready, 2)
                pe.wait_ge(oj_in, bg * (16 * NI * 4) + 16 * NI * 4)
                last = isinstance(bg, int) and bg == NBG - 1
                pe.wait_ge(proj_ready, (NBG - 1) * NI + 1 if last else w + 1)
                dst = last_ps[i] if last else out_ps
                for b in range(4):
                    ins = pe.matmul(dst[:, b * D:(b + 1) * D], OJ[:, i, b * P:(b + 1) * P], wo[:, :],
                                    start=True, stop=True)
                ins.then_inc(proj_ps, 1)

            def body(bg, turn):
                first, last = turn is None and bg == 0, turn is None and bg == NBG - 1
                uses = work_uses(bg, last)
                if isinstance(bg, int) and bg == 0:
                    before = [("qkvw", 1, 2), ("qkvw", 1, 3)]
                else:
                    before = [("oT", bg - 1, 2), ("oT", bg - 1, 3)]
                before += [(kind, n, j) for _, kind, n, j in uses]
                ffn, fold = ffn_tiles(bg, turn), folds(bg, turn)
                for q in range(NQ + 1):
                    for u, (qq, kind, n, j) in enumerate(uses):
                        if qq == q:
                            i = (q // 2 + 2) % NI
                            if kind == "qkvw" and i == 0 and j == 0:
                                pe.wait_ge(ready["xT"], bg * 4 + 8)
                            copied(*before[u])
                            fill(kind, n, j, u, i)
                    if q == NQ:
                        if last:
                            for i in range(NI):
                                project(bg, i)
                        break
                    for m in range(max(FFN_LOOP)):
                        if m < len(ffn[q]):
                            ffn_tile(*ffn[q][m])
                        if first and (q, m) == START_EXPERTS:
                            ffn_transpose(0, 0, 0)
                            ffn_transpose(1, 1, 0)
                            ffn_up(0, 0, 0)
                        if (q, m) in PROJECT_AT and not first:
                            project(bg - 1, PROJECT_AT.index((q, m)))
                        if m == SUM_BEHIND and (not last or q < NQ - 1):
                            sum_keys(bg * NQ + q + 1, q + 1, fold[q])

            bgs(pe, body)

        @block.vector
        def _(dve):
            own = Count(dve_own)

            def stats(g, s, m):
                if not (isinstance(g, int) and g == 0):
                    dve.wait_ge(var1, g)
                dve.wait_ge(x_in[s], (m + 1) * 16)
                for k in range(GT):
                    ins = dve.bn_stats(st[:, k, :], x_st[:, bass.ds(g * G + k * D, D)])
                own.step(dve, ins)
                dve.memset(idle[:, :], 0.0)
                for k in range(GT):
                    ins = dve.bn_aggr(mv[:, s, k, :], st[:, k, :])
                ins.then_inc(var1, 1)

            def norm(g, s, first=False):
                dve.wait_ge(dev1, g + 1)
                own.step(dve, dve.reciprocal(rs[:, s, :], dev[:, s, :]))
                own.inc(dve.scalar_tensor_tensor(out=nm[:, s, :], in0=mv[:, s, :, 0], scalar=-1.0, in1=rs[:, s, :],
                                                 op0=ALU.mult, op1=ALU.mult))
                own.step(dve, dve.tensor_tensor(sq[:, s, :], rs[:, s, :], rs[:, s, :], ALU.mult))
                dve.tensor_tensor(sq[:, s, :], sq[:, s, :], mv[:, s, :, 1], ALU.mult).then_inc(var2, 1)
                dve.tensor_copy(RS[:, bass.ds(g * GT, GT)], rs[:, s, :])
                dve.tensor_copy(NM[:, bass.ds(g * GT, GT)], nm[:, s, :])
                if not first:
                    dve.wait_ge(xnT_ps, g * 2 - 4)
                    dve.wait_ge(xhat_ready, g - 2)
                for k in range(GT):
                    ins = dve.tensor_scalar(xn_st[s][:, k, :], x_st[:, bass.ds(g * G + k * D, D)], rs[:, s, k:k + 1], nm[:, s, k:k + 1],
                                            ALU.mult, ALU.add)
                ins.then_inc(xn_ready, 1)

            def second_deviation(g, s):
                dve.wait_ge(dev_2, g + 1)
                dve.reciprocal(rs2[:, s, :], dev2[:, s, :]).then_inc(rs2_ready, 1)

            dve.wait_ge(consts, 8)
            stats(0, 0, 0)
            stats(1, 1, 0)
            norm(0, 0, True)
            stats(2, 2, 0)
            second_deviation(0, 0)
            norm(1, 1, True)
            stats(3, 0, 1)
            second_deviation(1, 1)
            norm(2, 2, True)
            with dve.Fori(1, (NG - 2) // 3) as it:
                own.turn(it - 1, 12)
                for j in range(1, 4):
                    stats(it * 3 + j, j % 3, it + j // 3)
                    second_deviation(it * 3 + j - 2, (j - 2) % 3)
                    norm(it * 3 + j - 1, (j - 1) % 3)
            own.left((NG - 2) // 3 - 1)
            stats(NG - 1, (NG - 1) % 3, (NG - 1) // 3)
            second_deviation(NG - 3, (NG - 3) % 3)
            norm(NG - 2, (NG - 2) % 3)
            second_deviation(NG - 2, (NG - 2) % 3)
            norm(NG - 1, (NG - 1) % 3)
            second_deviation(NG - 1, (NG - 1) % 3)

            dve.wait_ge(xbg_in, 16 * BGT // GT)
            own.step(dve, dve.memset(idle[:, :], 0.0))
            for t in range(BGT):
                ins = dve.tensor_scalar(x_bg[:, t, :], x_bg[:, t, :], RS[:, t:t + 1], NM[:, t:t + 1], ALU.mult, ALU.add)
            ins.then_inc(xnb_ready, 1)

            dve.wait_ge(sc_ready, NG)
            dve.tensor_reduce(mx, scores, AX_X, ALU.max).then_inc(mx_ready, 1)
            dve.wait_ge(mx_ready, 1)
            own.step(dve, dve.tensor_tensor(eq, scores, mx.unsqueeze(2).broadcast_to([P, NT, E]), ALU.is_ge))
            own.step(dve, dve.tensor_tensor(eq, eq, rank.unsqueeze(1).broadcast_to([P, NT, E]), ALU.mult))
            own.step(dve, dve.tensor_reduce(best, eq, AX_X, ALU.max))
            dve.tensor_tensor(ohb, eq, best.unsqueeze(2).broadcast_to([P, NT, E]), ALU.is_equal).then_inc(oh_ready, 1)
            dve.wait_ge(prefix_ps, 1)
            dve.tensor_tensor(ahead.rearrange("p (t e) -> p t e", e=E),
                              sums[1][0:NT, 0:E].unsqueeze(1).broadcast_to([NT, NT + 1, E]),
                              tri[0:NT, 0:NT + 1].unsqueeze(2).broadcast_to([NT, NT + 1, E]), ALU.mult)\
                .then_inc(ahead_ready, 1)
            dve.wait_ge(prefix_ps, 2)
            ahead_of = sums[0][:, :].rearrange("p (t e) -> p t e", e=E)
            own.step(dve, dve.tensor_scalar(tot_i[:, :], out_ps[:, 0:E], float(P - 1), None, ALU.add))
            own.step(dve, dve.tensor_scalar(tot_i[:, :], tot_i[:, :], P.bit_length() - 1, None, ALU.logical_shift_right))
            own.step(dve, dve.tensor_copy(tiles, tot_i[:, :]))
            src, dst = tiles, ends_a
            for sh in (1, 2, 4):
                own.inc(dve.tensor_copy(dst[:, 0:sh], src[:, 0:sh]))
                own.step(dve, dve.tensor_tensor(dst[:, sh:], src[:, sh:], src[:, 0:E - sh], ALU.add))
                src, dst = dst, (ends_b if dst is ends_a else ends_a)
            ends = src
            own.step(dve, dve.tensor_tensor(base, ends, tiles, ALU.subtract))
            own.step(dve, dve.tensor_scalar(base, base, float(P), None, ALU.mult))
            own.step(dve, dve.tensor_tensor(eq, ahead_of, base.unsqueeze(1).broadcast_to([P, NT, E]), ALU.add))
            own.step(dve, dve.tensor_tensor(eq, eq, ohb, ALU.mult))
            own.step(dve, dve.tensor_reduce(slot_f, eq, AX_X, ALU.add))
            dve.tensor_copy(slot[:, :], slot_f).then_inc(route_ready, 1)
            own.step(dve, dve.tensor_scalar(ids_f[:, :], tile_no[:, :], ends[:, 0:1], None, ALU.is_ge))
            for e in range(1, E - 1):
                own.step(dve, dve.scalar_tensor_tensor(out=ids_f[:, :], in0=tile_no[:, :], scalar=ends[:, e:e + 1],
                                                       in1=ids_f[:, :], op0=ALU.is_ge, op1=ALU.add))
            dve.tensor_copy(ids[:, :], ids_f[:, :]).then_inc(route_ready, 1)
            dve.wait_ge(emx_ready, 1)
            own.step(dve, dve.tensor_scalar(den, emx, 1.0, None, ALU.add))
            own.step(dve, dve.reciprocal(alpha[:, :], den))

            def view(t):
                return t.rearrange("p (g r h) -> p g r h", g=H, h=H)

            def keys(t):
                return t.rearrange("p r g -> p g r").unsqueeze(3).broadcast_to([P, H, HP, H])

            def queries(t):
                return t.unsqueeze(1).broadcast_to([P, H, HP, H])

            def scores_of(n, q):
                m, p0 = (q // 2) % 2, HP * (q % 2)
                if q % 2 == 0:
                    dve.wait_ge(ready["qkvw"], n * 2 + 4)
                if not (isinstance(n, int) and n == 0):
                    dve.wait_ge(exp_ready, n)
                if not (isinstance(n, int) and n < 3):
                    dve.wait_ge(f_ready, n - 2)
                for d, dst in ((0, A), (1, Bb)):
                    ins = dve.tensor_tensor(view(dst[:, :]), queries(QK[:, m, d, 0, p0:p0 + HP, :]),
                                            keys(QK[:, m, d, 1, p0:p0 + HP, :]), ALU.mult)
                own.step(dve, ins)
                own.step(dve, dve.tensor_tensor(A[:, :], A[:, :], Bb[:, :], ALU.add))
                own.step(dve, dve.tensor_reduce(Bb[:, 0:N], A[:, :].rearrange("p (g n) -> p n g", g=H), AX_X, ALU.max))
                dve.tensor_tensor(A[:, :].rearrange("p (g n) -> p g n", g=H), A[:, :].rearrange("p (g n) -> p g n", g=H),
                                  Bb[:, 0:N].unsqueeze(1).broadcast_to([P, H, N]), ALU.subtract).then_inc(s_ready, 1)

            def exp_v(n, q, folded=0):
                m, p0 = q // 2, HP * (q % 2)
                if q % 2 == 0:
                    dve.wait_ge(vw_ready, n * 2 + 4)
                dve.wait_ge(exp_ready, n + 1)
                if not (isinstance(n, int) and n < 2):
                    dve.wait_ge(sum_ready, n - 1)
                for d in range(2):
                    ins = dve.tensor_tensor(view(EXY[:, q % 2, 1 + d, :]), view(EXY[:, q % 2, 0, :]),
                                            keys(VW[:, m, d, 0, p0:p0 + HP, :]), ALU.mult)
                if folded:
                    own.step(dve, ins)
                    lo, hi = EXY[:, q % 2, 3 - folded:, 0:SZ // 2], EXY[:, q % 2, 3 - folded:, SZ // 2:]
                    ins = dve.tensor_tensor(lo, lo, hi, ALU.add)
                ins.then_inc(ev_ready, 1)

            def finish(bg, q):
                n = bg * NQ + q
                i, p0 = q // 2, HP * (q % 2)
                dve.wait_ge(sum_ready, n + 1)
                bank_ = sums[q % 2]
                own.step(dve, dve.reciprocal(rden[:, :], bank_[:, 0:N]))
                if isinstance(n, int) and n + 3 > NBG * NQ:
                    dve.wait_ge(s_ready, NBG * NQ)
                else:
                    dve.wait_ge(s_ready, n + 3)
                own.step(dve, dve.tensor_tensor(osb[:, :, :], bank_[:, N:3 * N].rearrange("p (d n) -> p d n", d=2),
                                                rden[:, :].unsqueeze(1).broadcast_to([P, 2, N]), ALU.mult))
                if q == 0 and not isinstance(bg, int) or q == 0 and bg:
                    dve.wait_ge(filled["oT"], bg * 4)
                dst = O[:, :, i * C + 2 * p0:i * C + 2 * p0 + 2 * HP].rearrange("p h (r d) -> p d r h", d=2)
                dve.tensor_tensor(dst, osb[:, :, :].rearrange("p d (r h) -> p d r h", h=H),
                                  VW[:, i, :, 1, p0:p0 + HP, :], ALU.mult).then_inc(f_ready, 1)

            dve.wait_ge(zeroed, 16 * ZERO_DMAS)
            scores_of(0, 0)
            scores_of(1, 1)
            dve.wait_ge(b1_ps, 1)
            w1v = W1s.rearrange("p (e c) -> p e c", e=E)
            dve.tensor_tensor(w1v[:, :, F:], out_ps[:, 0:E * FC].rearrange("p (e c) -> p e c", e=E),
                      b1T.rearrange("p (e c) -> p e c", e=E), ALU.add).then_inc(w1_ready, 1)
            exp_v(0, 0)

            def gate_in(bg, i):
                dve.wait_ge(fxn_ready, bg * NI + i + 1)
                for k in range(4):
                    t = bg * 4 + i * BGT + k
                    ins = dve.scalar_tensor_tensor(
                        out=fin_z[i][:, k * D:(k + 1) * D], in0=f_all[:, bass.ds(t * D, D)],
                        scalar=alpha[:, bass.ds(t, 1)], in1=fin_n[i][:, k * D:(k + 1) * D],
                        op0=ALU.mult, op1=ALU.add)
                ins.then_inc(z_ready, 1)

            def body(bg, turn):
                last, fold = turn is None and bg == NBG - 1, folds(bg, turn)
                for q in range(NQ):
                    if last and q == NQ - 1:
                        dve.wait_ge(exp_ready, NBG * NQ)
                        dve.wait_ge(gathered[0], 16 * BGT)
                        gate_in(0, 0)
                    if not last or q < NQ - 2:
                        scores_of(bg * NQ + q + 2, (q + 2) % NQ)
                    if not last or q < NQ - 1:
                        exp_v(bg * NQ + q + 1, (q + 1) % NQ, fold[q])
                    finish(bg, q)

            body(0, None)
            with dve.Fori(0, len(LOOP_BGS)) as turn:
                own.turn(turn, NQ * 6)
                body(turn + LOOP_BGS[0], turn)
            own.left(len(LOOP_BGS))
            body(NBG - 1, None)

            def gated(bg, i):
                w = bg * NI + i
                s = last_ps[i][:, :] if isinstance(bg, int) else s_all[:, bass.ds(w * NF, NF)]
                dve.wait_ge(sg_ready, w + 1)
                own.step(dve, dve.tensor_tensor(fin_z[i], fin_z[i], s, ALU.mult))
                dve.wait_ge(res_out[i], (bg + 1) * 16)
                dve.tensor_tensor(fin_r[i], fin_z[i], fin_x[i], ALU.add).then_inc(res_ready, 1)

            dve.wait_ge(gathered[1], 16 * (NT - BGT))
            dve.wait_ge(proj_ready, (NBG - 1) * NI + 1)
            with dve.Fori(0, NBG - 1) as bg:
                own.turn(bg, NI)
                for i in range(NI):
                    gate_in(bg + (i + 1) // NI, (i + 1) % NI)
                    gated(bg, i)
            own.left(NBG - 1)
            for i in range(NI):
                if i + 1 < NI:
                    gate_in(NBG - 1, i + 1)
                dve.wait_ge(proj_ps, (NBG - 1) * NI + i + 1)
                gated(NBG - 1, i)


INS = ['L0_attn_x', 'L0_attn_w_qkvw', 'L0_attn_w_out', 'L0_ffn_centroids', 'L0_ffn_gamma', 'L0_ffn_beta',
       'L0_ffn_W1', 'L0_ffn_b1', 'L0_ffn_W2', 'L0_ffn_b2']


def kernel(**inputs):
    import numpy as np
    import concourse.bacc as bacc
    from concourse.bass_utils import run_bass_kernel_spmd

    nc = bacc.Bacc("TRN2", target_bir_lowering=False, num_devices=1)
    arrays, args = {}, []
    for name in INS:
        a = np.ascontiguousarray(inputs[name])
        arrays[f"in_{name}"] = a
        args.append(nc.dram_tensor(f"in_{name}", a.shape, mybir.dt.from_np(a.dtype), kind="ExternalInput").ap())
    out = nc.dram_tensor("out", inputs["L0_attn_x"].shape, F32, kind="ExternalOutput").ap()
    program(nc, *args, out)
    r = run_bass_kernel_spmd(nc, [arrays], core_ids=[0])
    return r.results[0]["out"]
```
